# Optimizing a Trainium2 kernel written in Bass

```python
import numpy as np
import jax
import jax.numpy as jnp

def _softmax(x, axis=-1):
    return jax.nn.softmax(x, axis=axis)

def _gelu(x):
    return jax.nn.gelu(x, approximate=True)

def _silu(x):
    return jax.nn.silu(x)

def _sigmoid(x):
    return jax.nn.sigmoid(x)

def _layernorm(x, axis=-1, eps=1e-05):
    m = jnp.mean(x, axis=axis, keepdims=True)
    v = jnp.var(x, axis=axis, keepdims=True)
    return (x - m) / jnp.sqrt(v + eps)

def _scatter_add(tgt, idx, src, axis=0):
    return tgt.at[idx].add(src)

def _segment_sum(src, seg, n):
    return jax.ops.segment_sum(src, seg, n)
kernel_name = 'mk_gnn_preln_d2_gnn_r8_570a43'

def setup_inputs(seed: int=0):
    np.random.seed(seed)
    _w = jnp.asarray

    def _rec_inputs():
        import jax
        import jax.numpy as jnp
        _gk = jax.random.key(seed)
        x = -1.686e-05 + 1 * jax.random.normal(jax.random.fold_in(_gk, 1), (6250, 160), jnp.float32)
        src = jax.random.randint(jax.random.fold_in(_gk, 2), (100000,), 0, 6250, jnp.int32)
        dst = jax.random.randint(jax.random.fold_in(_gk, 3), (100000,), 0, 6250, jnp.int32)
        _o = jnp.argsort(dst, stable=True)
        src = src[_o]
        dst = dst[_o]
        edge_attr_16 = 6.40344e-05 + 1.00026 * jax.random.normal(jax.random.fold_in(_gk, 11), (100000, 16), jnp.float32)
        edge_attr_4 = 0.0007022 + 0.999661 * jax.random.normal(jax.random.fold_in(_gk, 12), (100000, 4), jnp.float32)
        node_vec1 = -0.00915711 + 0.999674 * jax.random.normal(jax.random.fold_in(_gk, 14), (6250, 1), jnp.float32)
        return (x, src, dst, edge_attr_16, edge_attr_4, node_vec1)
    x, src, dst, edge_attr_16, edge_attr_4, node_vec1 = _rec_inputs()

    def _L0_gnn_setup():
        import jax, jax.numpy as jnp
        import numpy as np
        MUL0, MUL1 = (64, 32)
        INV_SQRT3 = 1.0 / np.sqrt(3.0)

        def _split(x):
            return (x[:, :MUL0], x[:, MUL0:].reshape(x.shape[0], MUL1, 3))

        def _merge(o0, o1):
            return jnp.concatenate([o0, o1.reshape(o1.shape[0], -1)], axis=-1)

        def _tp(x0, x1, y0, y1, w000, w011, w101, w110):
            fan0 = x0.shape[1] * y0.shape[1] + x1.shape[1] * y1.shape[1]
            fan1 = x0.shape[1] * y1.shape[1] + x1.shape[1] * y0.shape[1]
            out0 = (jnp.einsum('eu,ev,uvw->ew', x0, y0, w000) + INV_SQRT3 * jnp.einsum('euk,evk,uvw->ew', x1, y1, w110)) / np.sqrt(fan0)
            out1 = (jnp.einsum('eu,evk,uvw->ewk', x0, y1, w011) + jnp.einsum('euk,ev,uvw->ewk', x1, y0, w101)) / np.sqrt(fan1)
            return (out0, out1)

        def _lin(x0, x1, w0, w1):
            return (x0 @ w0 / np.sqrt(x0.shape[1]), jnp.einsum('euk,uv->evk', x1, w1) / np.sqrt(x1.shape[1]))
        key = jax.random.key(seed)
        ks = jax.random.split(key, 20)
        N, E = (6250, 62500)
        inp = {'node_features': jax.random.normal(ks[0], (N, MUL0 + 3 * MUL1), dtype=jnp.float32), 'edge_index': jax.random.randint(ks[1], (2, E), 0, N, dtype=jnp.int64), 'edge_attr_tensor': jax.random.normal(ks[2], (E, 4), dtype=jnp.float32), 'node_attr_scalar_raw': jax.random.normal(ks[3], (N, 1), dtype=jnp.float32), 'wm000': jax.random.normal(ks[4], (MUL0, 1, MUL0), dtype=jnp.float32), 'wm011': jax.random.normal(ks[5], (MUL0, 1, MUL1), dtype=jnp.float32), 'wm101': jax.random.normal(ks[6], (MUL1, 1, MUL1), dtype=jnp.float32), 'wm110': jax.random.normal(ks[7], (MUL1, 1, MUL0), dtype=jnp.float32), 'lm0': jax.random.normal(ks[8], (MUL0, MUL0), dtype=jnp.float32), 'lm1': jax.random.normal(ks[9], (MUL1, MUL1), dtype=jnp.float32), 'wu000': jax.random.normal(ks[10], (MUL0, MUL0, MUL0), dtype=jnp.float32), 'wu011': jax.random.normal(ks[11], (MUL0, MUL1, MUL1), dtype=jnp.float32), 'wu101': jax.random.normal(ks[12], (MUL1, MUL0, MUL1), dtype=jnp.float32), 'wu110': jax.random.normal(ks[13], (MUL1, MUL1, MUL0), dtype=jnp.float32), 'lu0': jax.random.normal(ks[14], (MUL0, MUL0), dtype=jnp.float32), 'lu1': jax.random.normal(ks[15], (MUL1, MUL1), dtype=jnp.float32)}
        return inp
    _L0_gnn_all = _L0_gnn_setup()
    _L0_gnn_in = {k: v for k, v in _L0_gnn_all.items() if k in ('wm000', 'wm011', 'wm101', 'wm110', 'lm0', 'lm1', 'wu000', 'wu011', 'wu101', 'wu110', 'lu0', 'lu1')}
    del _L0_gnn_all

    def _L1_gnn_setup():
        import jax, jax.numpy as jnp
        import numpy as np
        N_NODES = 12500
        N_EDGES = 100000
        MUL_S = 64
        MUL_V = 32
        DIM = MUL_S + 3 * MUL_V
        EDGE_SCALAR_DIM = 16
        ISQ3 = 1.0 / np.sqrt(3.0)
        ISQ2 = 1.0 / np.sqrt(2.0)

        def _forward(x, edge_index, edge_feat, edge_scalars, W_ss, W_sv, W_vs, W_vv, W_rad, b_rad, L_s, L_v):
            src, dst = (edge_index[0], edge_index[1])
            n = x.shape[0]
            xs = x[:, :MUL_S]
            xv = x[:, MUL_S:].reshape(n, MUL_V, 3)
            xs_e = xs[src]
            xv_e = xv[src]
            es = edge_feat[:, 0]
            ev = edge_feat[:, 1:4]
            out_s = (jnp.einsum('eu,uo->eo', xs_e * es[:, None], W_ss) / np.sqrt(MUL_S) + jnp.einsum('eud,ed,uo->eo', xv_e, ev, W_vv) * ISQ3 / np.sqrt(MUL_V)) * ISQ2
            out_v = (jnp.einsum('eu,ed,uv->evd', xs_e, ev, W_sv) * ISQ3 / np.sqrt(MUL_S) + jnp.einsum('eud,e,uv->evd', xv_e, es, W_vs) * ISQ3 / np.sqrt(MUL_V)) * ISQ2
            messages = jnp.concatenate([out_s, out_v.reshape(-1, 3 * MUL_V)], axis=1)
            scale = jax.nn.sigmoid(edge_scalars @ W_rad.T + b_rad)
            messages = messages * scale
            agg = jax.ops.segment_sum(messages, dst, num_segments=n)
            h = x + agg
            hs = h[:, :MUL_S]
            hv = h[:, MUL_S:].reshape(n, MUL_V, 3)
            ys = hs @ L_s / np.sqrt(MUL_S)
            yv = jnp.einsum('nud,uv->nvd', hv, L_v) / np.sqrt(MUL_V)
            return jnp.concatenate([ys, yv.reshape(n, 3 * MUL_V)], axis=1)
        key = jax.random.key(seed)
        ks = jax.random.split(key, 12)
        x = jax.random.normal(ks[0], (N_NODES, DIM), dtype=jnp.float32)
        edge_index = jax.random.randint(ks[1], (2, N_EDGES), 0, N_NODES, dtype=jnp.int64)
        edge_feat = jax.random.normal(ks[2], (N_EDGES, 4), dtype=jnp.float32)
        edge_scalars = jax.random.normal(ks[3], (N_EDGES, EDGE_SCALAR_DIM), dtype=jnp.float32)
        W_ss = jax.random.normal(ks[4], (MUL_S, MUL_S), dtype=jnp.float32)
        W_sv = jax.random.normal(ks[5], (MUL_S, MUL_V), dtype=jnp.float32)
        W_vs = jax.random.normal(ks[6], (MUL_V, MUL_V), dtype=jnp.float32)
        W_vv = jax.random.normal(ks[7], (MUL_V, MUL_S), dtype=jnp.float32)
        W_rad = jax.random.normal(ks[8], (DIM, EDGE_SCALAR_DIM), dtype=jnp.float32) / np.sqrt(EDGE_SCALAR_DIM)
        b_rad = jax.random.normal(ks[9], (DIM,), dtype=jnp.float32) * 0.1
        L_s = jax.random.normal(ks[10], (MUL_S, MUL_S), dtype=jnp.float32)
        L_v = jax.random.normal(ks[11], (MUL_V, MUL_V), dtype=jnp.float32)
        return {'x': x, 'edge_index': edge_index, 'edge_feat': edge_feat, 'edge_scalars': edge_scalars, 'W_ss': W_ss, 'W_sv': W_sv, 'W_vs': W_vs, 'W_vv': W_vv, 'W_rad': W_rad, 'b_rad': b_rad, 'L_s': L_s, 'L_v': L_v}
    _L1_gnn_all = _L1_gnn_setup()
    _L1_gnn_in = {k: v for k, v in _L1_gnn_all.items() if k in ('W_ss', 'W_sv', 'W_vs', 'W_vv', 'W_rad', 'b_rad', 'L_s', 'L_v')}
    del _L1_gnn_all
    return {'x': x, 'src': src, 'dst': dst, 'edge_attr_16': edge_attr_16, 'edge_attr_4': edge_attr_4, 'node_vec1': node_vec1, 'L0_gnn_wm000': _L0_gnn_in['wm000'], 'L0_gnn_wm011': _L0_gnn_in['wm011'], 'L0_gnn_wm101': _L0_gnn_in['wm101'], 'L0_gnn_wm110': _L0_gnn_in['wm110'], 'L0_gnn_lm0': _L0_gnn_in['lm0'], 'L0_gnn_lm1': _L0_gnn_in['lm1'], 'L0_gnn_wu000': _L0_gnn_in['wu000'], 'L0_gnn_wu011': _L0_gnn_in['wu011'], 'L0_gnn_wu101': _L0_gnn_in['wu101'], 'L0_gnn_wu110': _L0_gnn_in['wu110'], 'L0_gnn_lu0': _L0_gnn_in['lu0'], 'L0_gnn_lu1': _L0_gnn_in['lu1'], 'L1_gnn_W_ss': _L1_gnn_in['W_ss'], 'L1_gnn_W_sv': _L1_gnn_in['W_sv'], 'L1_gnn_W_vs': _L1_gnn_in['W_vs'], 'L1_gnn_W_vv': _L1_gnn_in['W_vv'], 'L1_gnn_W_rad': _L1_gnn_in['W_rad'], 'L1_gnn_b_rad': _L1_gnn_in['b_rad'], 'L1_gnn_L_s': _L1_gnn_in['L_s'], 'L1_gnn_L_v': _L1_gnn_in['L_v']}

def reference(x, src, dst, edge_attr_16, edge_attr_4, node_vec1, L0_gnn_wm000, L0_gnn_wm011, L0_gnn_wm101, L0_gnn_wm110, L0_gnn_lm0, L0_gnn_lm1, L0_gnn_wu000, L0_gnn_wu011, L0_gnn_wu101, L0_gnn_wu110, L0_gnn_lu0, L0_gnn_lu1, L1_gnn_W_ss, L1_gnn_W_sv, L1_gnn_W_vs, L1_gnn_W_vv, L1_gnn_W_rad, L1_gnn_b_rad, L1_gnn_L_s, L1_gnn_L_v):
    import jax
    import jax.numpy as jnp

    def _L0_gnn_ref(node_features, edge_index, edge_attr_tensor, node_attr_scalar_raw, wm000, wm011, wm101, wm110, lm0, lm1, wu000, wu011, wu101, wu110, lu0, lu1):
        import jax, jax.numpy as jnp
        import numpy as np
        MUL0, MUL1 = (64, 32)
        INV_SQRT3 = 1.0 / np.sqrt(3.0)

        def _split(x):
            return (x[:, :MUL0], x[:, MUL0:].reshape(x.shape[0], MUL1, 3))

        def _merge(o0, o1):
            return jnp.concatenate([o0, o1.reshape(o1.shape[0], -1)], axis=-1)

        def _tp(x0, x1, y0, y1, w000, w011, w101, w110):
            fan0 = x0.shape[1] * y0.shape[1] + x1.shape[1] * y1.shape[1]
            fan1 = x0.shape[1] * y1.shape[1] + x1.shape[1] * y0.shape[1]
            out0 = (jnp.einsum('eu,ev,uvw->ew', x0, y0, w000) + INV_SQRT3 * jnp.einsum('euk,evk,uvw->ew', x1, y1, w110)) / np.sqrt(fan0)
            out1 = (jnp.einsum('eu,evk,uvw->ewk', x0, y1, w011) + jnp.einsum('euk,ev,uvw->ewk', x1, y0, w101)) / np.sqrt(fan1)
            return (out0, out1)

        def _lin(x0, x1, w0, w1):
            return (x0 @ w0 / np.sqrt(x0.shape[1]), jnp.einsum('euk,uv->evk', x1, w1) / np.sqrt(x1.shape[1]))
        N = node_features.shape[0]
        row, col = (edge_index[0], edge_index[1])
        r_vec = edge_attr_tensor[:, :3]
        dist = edge_attr_tensor[:, 3:4]
        e0 = dist
        e1 = r_vec[:, None, :]
        xj0, xj1 = _split(node_features[col])
        m0, m1 = _tp(xj0, xj1, e0, e1, wm000, wm011, wm101, wm110)
        d0, d1 = _lin(xj0, xj1, lm0, lm1)
        msgs = _merge(m0 + d0, m1 + d1)
        agg = jax.ops.segment_sum(msgs, row, num_segments=N)
        a0, a1 = _split(agg)
        x0, x1 = _split(node_features)
        u0, u1 = _tp(x0, x1, a0, a1, wu000, wu011, wu101, wu110)
        ud0, ud1 = _lin(x0, x1, lu0, lu1)
        return node_features + _merge(u0 + ud0, u1 + ud1)

    def _L1_gnn_ref(x, edge_index, edge_feat, edge_scalars, W_ss, W_sv, W_vs, W_vv, W_rad, b_rad, L_s, L_v):
        import jax, jax.numpy as jnp
        import numpy as np
        N_NODES = 12500
        N_EDGES = 100000
        MUL_S = 64
        MUL_V = 32
        DIM = MUL_S + 3 * MUL_V
        EDGE_SCALAR_DIM = 16
        ISQ3 = 1.0 / np.sqrt(3.0)
        ISQ2 = 1.0 / np.sqrt(2.0)

        def _forward(x, edge_index, edge_feat, edge_scalars, W_ss, W_sv, W_vs, W_vv, W_rad, b_rad, L_s, L_v):
            src, dst = (edge_index[0], edge_index[1])
            n = x.shape[0]
            xs = x[:, :MUL_S]
            xv = x[:, MUL_S:].reshape(n, MUL_V, 3)
            xs_e = xs[src]
            xv_e = xv[src]
            es = edge_feat[:, 0]
            ev = edge_feat[:, 1:4]
            out_s = (jnp.einsum('eu,uo->eo', xs_e * es[:, None], W_ss) / np.sqrt(MUL_S) + jnp.einsum('eud,ed,uo->eo', xv_e, ev, W_vv) * ISQ3 / np.sqrt(MUL_V)) * ISQ2
            out_v = (jnp.einsum('eu,ed,uv->evd', xs_e, ev, W_sv) * ISQ3 / np.sqrt(MUL_S) + jnp.einsum('eud,e,uv->evd', xv_e, es, W_vs) * ISQ3 / np.sqrt(MUL_V)) * ISQ2
            messages = jnp.concatenate([out_s, out_v.reshape(-1, 3 * MUL_V)], axis=1)
            scale = jax.nn.sigmoid(edge_scalars @ W_rad.T + b_rad)
            messages = messages * scale
            agg = jax.ops.segment_sum(messages, dst, num_segments=n)
            h = x + agg
            hs = h[:, :MUL_S]
            hv = h[:, MUL_S:].reshape(n, MUL_V, 3)
            ys = hs @ L_s / np.sqrt(MUL_S)
            yv = jnp.einsum('nud,uv->nvd', hv, L_v) / np.sqrt(MUL_V)
            return jnp.concatenate([ys, yv.reshape(n, 3 * MUL_V)], axis=1)
        return _forward(x, edge_index, edge_feat, edge_scalars, W_ss, W_sv, W_vs, W_vv, W_rad, b_rad, L_s, L_v)
    edge_index = jnp.stack([src, dst])
    h = jnp.maximum(_layernorm(x, axis=-1), 0.0)
    x = x + _L0_gnn_ref(h, edge_index, edge_attr_4, node_vec1, L0_gnn_wm000, L0_gnn_wm011, L0_gnn_wm101, L0_gnn_wm110, L0_gnn_lm0, L0_gnn_lm1, L0_gnn_wu000, L0_gnn_wu011, L0_gnn_wu101, L0_gnn_wu110, L0_gnn_lu0, L0_gnn_lu1)
    h = jnp.maximum(_layernorm(x, axis=-1), 0.0)
    x = x + _L1_gnn_ref(h, edge_index, edge_attr_4, edge_attr_16, L1_gnn_W_ss, L1_gnn_W_sv, L1_gnn_W_vs, L1_gnn_W_vv, L1_gnn_W_rad, L1_gnn_b_rad, L1_gnn_L_s, L1_gnn_L_v)
    return x

_drawn_inputs = setup_inputs


def setup_inputs(seed=0):
    import zlib

    import numpy as np

    out = dict(_drawn_inputs(seed))
    spreads = {}
    factors = {'L1_gnn_b_rad': 6.324}
    for name, (base, spread) in spreads.items():
        noise = np.random.default_rng([zlib.crc32(name.encode()), seed]).standard_normal(out[name].shape)
        drawn = base * np.exp(spread * noise) if base else spread * noise
        out[name] = jnp.asarray(drawn.astype(out[name].dtype))
    for name, factor in factors.items():
        out[name] = (out[name] * factor).astype(out[name].dtype)
    return out
```

```python
from contextlib import ExitStack

import concourse.bass as bass
from concourse import mybir
import numpy as np

P = 128
N, E = 6250, 100000
F, S, V = 160, 64, 32
NB = -(-N // P)
NBE = NB + NB % 2
NN = NB * P
EC = -(-E // P)
EN = EC * P
SW = 2 * P
SLOTS = 4
W = (EN + NB * (SW - 1)) // SW
W = -(-W // SLOTS) * SLOTS
Q = -(-W // P)
R0, R1 = 8, 32
CH = 17
PIECES = EC // CH
assert PIECES * CH == EC and PIECES % 2 == 0
A0 = F + F + 3 * S + 3 * V
HALF = A0 // 2
TW = 384
KC = -(-A0 // P)
WB, WT, WU, WF, WG, W110 = 0, KC * F, KC * F + 2 * TW, KC * F + 2 * TW + 2 * F, KC * F + 2 * TW + 4 * F, KC * F + 2 * TW + 5 * F
WS = W110 + 8 * S
C_ID, C_TRI, C_ONE, C_IOTA, C_WIN = 0, P, 2 * P, 3 * P, 4 * P
CW = 4 * P + Q
EPS = 1e-5


def program(nc, xin, rec0, rec1, key0, key1, wsmall, wscale, wbig, const, out):
    f32, i32 = mybir.dt.float32, mybir.dt.int32
    ALU, ACT, AX = mybir.AluOpType, mybir.ActivationFunctionType, mybir.AxisListType
    ds = bass.ds
    ctx = ExitStack()
    with ctx:
        ctx.enter_context(nc.allow_non_contiguous_dma(reason="short tables"))

        def sb(name, shape, dt=f32):
            return ctx.enter_context(nc.sbuf_tensor(name, shape, dt))

        def sem(name):
            return ctx.enter_context(nc.semaphore(name))

        hD = nc.dram_tensor("h_rows", [NN, F], f32).ap()
        tD = nc.dram_tensor("t_rows", [NN, TW], f32).ap()
        x2D = nc.dram_tensor("x2_rows", [NN, F], f32).ap()
        posD = [nc.dram_tensor(f"pos{l}", [P, EC], i32).ap() for l in range(2)]
        eD = [nc.dram_tensor(f"sorted{l}", [EN + SW, r], i32).ap() for l, r in ((0, R0), (1, R1))]
        tabD = [nc.dram_tensor(f"windows{l}", [2, Q * P], i32).ap() for l in range(2)]
        baseD = [nc.dram_tensor(f"bases{l}", [1, Q * P], f32).ap() for l in range(2)]

        acc = sb("acc", [P, NB * A0])
        acc1 = acc[:, 0:NB * F]
        hS = sb("hS", [P, NB, F])
        RW = 9392
        room = sb("room", [P, RW])
        ws = sb("ws", [P, WS])
        cst = sb("cst", [P, CW])
        base = sb("base", [P, W])
        tab = sb("tab", [1, 2 * W], i32)
        rw0 = sb("rw0", [P, SLOTS, 2, R0], i32)
        rw1 = sb("rw1", [P, SLOTS, 2 * R1], i32)
        srec = sb("srec", [P, 2, CH * R1], i32)
        spos = sb("spos", [P, 2, CH], i32)
        keyf = sb("keyf", [P, SLOTS, 2])
        ps = ctx.enter_context(nc.psum_tensor("ps", [P, 8, 512], f32))

        ident, tri, ones, iota = (cst[:, c:c + P] for c in (C_ID, C_TRI, C_ONE, C_IOTA))

        at = [0]

        def early(words):
            at[0] += words
            return acc[:, at[0] - words:at[0]]

        keys, blki, blkf, rank, posi = (early(EC) for _ in range(5))
        eq = [early(EC) for _ in range(2)]
        run = [early(EC) for _ in range(2)]
        scl = early(WS)
        xs = early(NB * F).rearrange("p (b f) -> p b f", f=F)
        tail = early(2 * R1).bitcast(i32)
        cnt, off, tot, incl, exc, nwin, nwi, wend, pad, mask, junk = (early(NBE) for _ in range(11))
        stats = early(NB * 6).rearrange("p (b s) -> p b s", s=6)
        mean, var, tmpn, rstd = (early(NB) for _ in range(4))
        wb_, wst, wpad, wbase = (early(Q) for _ in range(4))
        wsti, wbi = (early(Q).bitcast(i32) for _ in range(2))
        assert at[0] <= NB * A0

        in_key = [sem(f"in_key{l}") for l in range(2)]
        in_x, in_c, in_ws = sem("in_x"), sem("in_c"), sem("in_ws")
        cnt_ready, off_ready = sem("cnt_ready"), sem("off_ready")
        pos_ready, pos_stored = sem("pos_ready"), sem("pos_stored")
        tabs_ready, tabs_stored = sem("tabs_ready"), sem("tabs_stored")
        tail_ready, tail_stored = sem("tail_ready"), sem("tail_stored")
        var_ready, std_ready = sem("var_ready"), sem("std_ready")
        h_ready, h_stored = sem("h_ready"), sem("h_stored")
        acc_clear = sem("acc_clear")
        dv = sem("dv")
        dv_cnt = [sem(f"dv_cnt{l}") for l in range(2)]
        dv_rank = [sem(f"dv_rank{l}") for l in range(2)]
        dv_bn = sem("dv_bn")
        piece = [[sem(f"piece{l}{h}") for h in range(2)] for l in range(2)]
        sent = [[sem(f"sent{l}{h}") for h in range(2)] for l in range(2)]
        tab_in = sem("tab_in")
        pool_go = sem("pool_go")
        rec_in = [[sem(f"rec_in{l}{s}") for s in range(SLOTS)] for l in range(2)]
        row_in = [[sem(f"row_in{l}{s}") for s in range(SLOTS)] for l in range(2)]
        key_done = [sem(f"key_done{l}") for l in range(2)]
        scaled = [sem(f"scaled{l}") for l in range(2)]
        built = [sem(f"built{l}") for l in range(2)]
        summed = [sem(f"summed{l}") for l in range(2)]
        added = [sem(f"added{l}") for l in range(2)]
        attr_t, attr_c, gate_mm, gate_done = sem("attr_t"), sem("attr_c"), sem("gate_mm"), sem("gate_done")
        msg = sem("msg")
        wbig_in, u_x_in = sem("wbig_in"), sem("u_x_in")
        agg_c, agg_t, agg_t_sb, agg_mm, agg_sb = sem("agg_c"), sem("agg_t"), sem("agg_t_sb"), sem("agg_mm"), sem("agg_sb")
        h_t, h_t_sb, z1_mm, z1_used = sem("h_t"), sem("h_t_sb"), sem("z1_mm"), sem("z1_used")
        z0_mm, z0_prod, z0_sum = sem("z0_mm"), sem("z0_prod"), sem("z0_sum")
        g_done, g_t, g_t_sb, out_mm = sem("g_done"), sem("g_t"), sem("g_t_sb"), sem("out_mm")
        y_done, u_var, u_std, h2_done = sem("y_done"), sem("u_var"), sem("u_std"), sem("h2_done")
        h2_kept, h2_t, h2_t_sb, t_mm, t_sb = sem("h2_kept"), sem("h2_t"), sem("h2_t_sb"), sem("t_mm"), sem("t_sb")
        u_dve = sem("u_dve")
        u_t_out, u_x2_out = sem("u_t_out"), sem("u_x2_out")
        f_x_in, f_pe, f_act, f_dve, f_out = sem("f_x_in"), sem("f_pe"), sem("f_act"), sem("f_dve"), sem("f_out")

        xu = room[:, 0:SLOTS * 2 * A0].rearrange("p (s c f) -> p s c f", s=SLOTS, c=2)
        oh = room[:, SLOTS * 2 * A0:SLOTS * 2 * (A0 + P)].rearrange("p (s c f) -> p s c f", s=SLOTS, c=2)
        at[0] = 0

        def part(words):
            at[0] += words
            assert at[0] <= RW
            return room[:, at[0] - words:at[0]]

        tb = part(SLOTS * 2 * TW).rearrange("p (s c f) -> p s c f", s=SLOTS, c=2)
        oh1 = part(2 * 2 * P).rearrange("p (s c f) -> p s c f", s=2, c=2)
        mg = part(2 * 2 * F).rearrange("p (s c f) -> p s c f", s=2, c=2)
        gt = part(2 * 2 * F).rearrange("p (s f) -> p s f", s=2)
        atr = part(2 * P).rearrange("p (s f) -> p s f", s=2)
        at[0] = 0
        w000 = part(S * S)
        w1x1 = part(V * V)
        prod = part(1024)
        aT = prod[:, 0:KC * P]
        aS, cat, catT = part(F), part(P), part(P)
        hT = part(2 * P)
        g, g2 = part(1024), part(1024)
        gT = g2
        ab = g2[:, 0:A0]
        hb = prod[:, KC * P:KC * P + F]
        tS = g[:, 0:TW]
        xb, y = part(F), part(F)
        o1 = part(2 * 3 * V)
        st6, mv = part(6), part(4)
        fh, fT, fo, fx = (room[:, k * 512:k * 512 + n] for k, n in ((0, F), (1, 2 * P), (2, F), (3, F)))

        def loop(eng, n0, n1):
            return eng.Fori(n0, n1)

        block = ctx.enter_context(nc.Block())

        def send(sp, l):
            r, rec = ((R0, rec0), (R1, rec1))[l]
            sp.wait_ge(pos_stored, 16 * (l + 1))

            def one(j, h, first):
                k = j * 2 + h
                if not first:
                    sp.wait_ge(pos_stored, 16 * (l + 1))
                    sp.wait_ge(sent[l][h], j * (16 * CH))
                sp.dma_start(spos[:, h, :], posD[l][:, ds(k * CH, CH)]).then_inc(piece[l][h], 16)
                sp.dma_start(srec[:, h, 0:CH * r], rec[:, ds(k * (CH * r), CH * r)]).then_inc(piece[l][h], 16)

            for h in range(2):
                one(0, h, True)
            with loop(sp, 1, PIECES // 2) as j:
                for h in range(2):
                    one(j, h, False)

        def load_tables(sp, l):
            sp.wait_ge(tabs_stored, 48 * (l + 1))
            if l == 1:
                sp.wait_ge(added[0], W)
            sp.dma_start(tab[0:1, 0:W], tabD[l][0:1, 0:W]).then_inc(tab_in, 16)
            sp.dma_start(tab[0:1, W:2 * W], tabD[l][1:2, 0:W]).then_inc(tab_in, 16)
            sp.dma_start(base[:, :], baseD[l][0:1, 0:W].to_broadcast((P, W))).then_inc(tab_in, 16)
            sp.wait_ge(tab_in, 48 * (l + 1))
            sp.wait_ge(tail_stored, 32)
            for h in range(2):
                sp.wait_ge(sent[l][h], 16 * CH * (PIECES // 2))

        def windows(sp, l):
            r = (R0, R1)[l]

            def one(it, s, first):
                w = it * SLOTS + s
                start = sp.value_load(tab[0:1, ds(w, 1)], min_val=0, max_val=EN)
                if not first:
                    sp.wait_ge((summed[0], msg)[l], w - SLOTS + 1)
                dst = rw0[:, s, :, :].rearrange("p c r -> p (c r)") if l == 0 else rw1[:, s, :]
                sp.dma_start(dst, eD[l][ds(start, SW), :].rearrange("(p c) r -> p (c r)", c=2)).then_inc(rec_in[l][s], 16)

            for s in range(SLOTS):
                one(0, s, True)
            with loop(sp, 1, W // SLOTS) as it:
                for s in range(SLOTS):
                    one(it, s, False)

        def nodes_io(sp):
            def one(b, first):
                if not first:
                    sp.wait_ge(y_done, b)
                sp.dma_start(xb, xin[ds(b * P, P), :]).then_inc(u_x_in, 16)
                sp.wait_ge(y_done, b + 1)
                sp.dma_start(x2D[ds(b * P, P), :], y).then_inc(u_x2_out, 16)
                sp.wait_ge(t_sb, b + 1)
                sp.dma_start(tD[ds(b * P, P), :], tS).then_inc(u_t_out, 16)

            one(0, True)
            with loop(sp, 1, NB) as b:
                one(b, False)

        @block.sync
        def _(sp):
            sp.dma_start(keys.bitcast(i32), key0).then_inc(in_key[0], 16)
            sp.dma_start(cst[:, :], const).then_inc(in_c, 16)
            sp.dma_start(xs, xin.rearrange("(b p) f -> p b f", p=P)).then_inc(in_x, 16)
            sp.dma_start(ws[:, :], wsmall).then_inc(in_ws, 16)
            sp.dma_start(scl, wscale).then_inc(in_ws, 16)
            sp.wait_ge(tail_ready, 3)
            for l, r in ((0, R0), (1, R1)):
                sp.dma_start(eD[l][EN:EN + SW, :].rearrange("(p c) r -> p (c r)", c=2),
                             tail[:, 0:2 * r]).then_inc(tail_stored, 16)
            for l in range(2):
                sp.wait_ge(pos_ready, l + 1)
                sp.dma_start(posD[l], posi.bitcast(i32)).then_inc(pos_stored, 16)
                sp.wait_ge(tabs_ready, l + 1)
                sp.dma_start(tabD[l][0, :].rearrange("(q p) -> p q", p=P), wsti).then_inc(tabs_stored, 16)
                sp.dma_start(tabD[l][1, :].rearrange("(q p) -> p q", p=P), wbi).then_inc(tabs_stored, 16)
                sp.dma_start(baseD[l][0, :].rearrange("(q p) -> p q", p=P), wbase).then_inc(tabs_stored, 16)
                if l == 0:
                    sp.dma_start(keys.bitcast(i32), key1).then_inc(in_key[1], 16)
                    sp.wait_ge(h_ready, 1)
                    sp.dma_start(hD.rearrange("(b p) f -> p b f", p=P), hS[:, :, :]).then_inc(h_stored, 16)
                    send(sp, 0)
            load_tables(sp, 0)
            windows(sp, 0)
            sp.wait_ge(summed[0], W)
            sp.dma_start(room[:, 0:S * S + V * V], wbig).then_inc(wbig_in, 16)
            nodes_io(sp)
            sp.wait_ge(u_t_out, 16 * NB)
            load_tables(sp, 1)
            windows(sp, 1)
            sp.wait_ge(u_x2_out, 16 * NB)

            def block_in(b, first):
                if not first:
                    sp.wait_ge(f_dve, b * 4)
                sp.dma_start(fx, x2D[ds(b * P, P), :]).then_inc(f_x_in, 16)
                sp.wait_ge(f_dve, (b + 1) * 4)
                sp.dma_start(out[ds(b * P, P), :], fo).then_inc(f_out, 16)

            sp.wait_ge(added[1], W)
            block_in(0, True)
            with loop(sp, 1, NB) as b:
                block_in(b, False)
            sp.wait_ge(f_out, 16 * NB)

        @block.gpsimd
        def _(pool):
            def scatter(l, load):
                r = (R0, R1)[l]

                def one(j, h):
                    pool.wait_ge(piece[l][h], (j + 1) * 32)
                    pool.sem_inc(pool_go, 1)
                    for k in range(CH):
                        nc.gpsimd.indirect_dma_start(
                            out=eD[l], out_offset=bass.IndirectOffsetOnAxis(ap=spos[:, h, k:k + 1], axis=0),
                            in_=srec[:, h, k * r:(k + 1) * r], in_offset=None).then_inc(sent[l][h], 16)

                if load:
                    def fetch(j, h, first):
                        k = j * 2 + h
                        if not first:
                            pool.wait_ge(sent[l][h], j * (16 * CH))
                        pool.dma_start(spos[:, h, :], posD[l][:, ds(k * CH, CH)]).then_inc(piece[l][h], 16)
                        pool.dma_start(srec[:, h, 0:CH * r], rec1[:, ds(k * (CH * r), CH * r)]).then_inc(piece[l][h], 16)

                    pool.wait_ge(pos_stored, 32)
                    for h in range(2):
                        pool.wait_ge(sent[0][h], 16 * CH * (PIECES // 2))
                    fetch(0, 0, True)
                    fetch(0, 1, True)
                    one(0, 0)
                    with loop(pool, 1, PIECES // 2) as j:
                        fetch(j, 0, False)
                        one(j - 1, 1)
                        fetch(j, 1, False)
                        one(j, 0)
                    one(PIECES // 2 - 1, 1)
                    for h in range(2):
                        pool.wait_ge(sent[l][h], 16 * CH * (PIECES // 2))
                else:
                    with loop(pool, 0, PIECES // 2) as j:
                        for h in range(2):
                            one(j, h)

            def gather(l):
                table = (hD, tD)[l]

                def one(it, s, first):
                    w = it * SLOTS + s
                    pool.wait_ge(rec_in[l][s], (it + 1) * 16)
                    if not first:
                        pool.wait_ge((summed[0], msg)[l], w - SLOTS + 1)
                    pool.sem_inc(pool_go, 1)
                    for c in range(2):
                        if l == 0:
                            dst, idx = xu[:, s, c, 0:F], rw0[:, s, c, 0:1]
                        else:
                            dst, idx = tb[:, s, c, :], rw1[:, s, c * R1:c * R1 + 1]
                        nc.gpsimd.indirect_dma_start(
                            out=dst, out_offset=None, in_=table,
                            in_offset=bass.IndirectOffsetOnAxis(ap=idx, axis=0)).then_inc(row_in[l][s], 16)

                for s in range(SLOTS):
                    one(0, s, True)
                with loop(pool, 1, W // SLOTS) as it:
                    for s in range(SLOTS):
                        one(it, s, False)

            scatter(0, False)
            pool.wait_ge(h_stored, 16)
            gather(0)
            scatter(1, True)
            pool.wait_ge(u_t_out, 16 * NB)
            pool.wait_ge(u_x2_out, 16 * NB)
            gather(1)

        @block.vector
        def _(dve):
            v = nc.vector

            class Steps:
                def __init__(self, s, start=0):
                    self.s, self.n, self.start = s, 0, start

                def inc(self, ins):
                    self.n += 1
                    ins.then_inc(self.s, 1)

                def link(self, ins):
                    self.inc(ins)
                    dve.wait_ge(self.s, self.start + self.n)

            c = Steps(dv)
            c.inc(v.memset(tail, 0))
            dve.wait_ge(dv, 1)
            for k in (1, R0 + 1, R1 + 1):
                v.memset(tail[:, k:k + 1], 2 * NN).then_inc(tail_ready, 1)

            def ranks(l):
                dve.wait_ge(in_key[l], 16)
                if l:
                    dve.wait_ge(pos_stored, 16)
                    dve.wait_ge(tabs_stored, 48)
                c.link(v.tensor_scalar(blki.bitcast(i32), keys.bitcast(i32), 7, None, ALU.arith_shift_right))
                c.link(v.tensor_copy(blkf, blki.bitcast(i32)))
                v.memset(junk[:, 2:3], 0.0).then_inc(dv_cnt[l], 1)
                with loop(dve, 0, NBE) as b:
                    dve.wait_ge(dv_cnt[l], b + 1)
                    v.tensor_scalar(eq[0], blkf, iota[:, ds(b, 1)], 0.0, ALU.is_equal, ALU.add,
                                    accum_out=cnt[:, ds(b, 1)]).then_inc(dv_cnt[l], 1)
                dve.wait_ge(dv_cnt[l], NBE + 1)
                c.inc(v.memset(junk[:, 0:1], 0.0))
                dve.wait_ge(dv, c.n)
                v.memset(junk[:, 0:1], 0.0).then_inc(cnt_ready, 1)
                dve.wait_ge(off_ready, l + 1)
                c.link(v.tensor_copy(tot, ps[:, 0, 64:64 + NBE]))
                c.link(v.tensor_tensor_scan(incl, ones[:, 0:NBE], tot, 0.0, ALU.mult, ALU.add))
                c.link(v.tensor_tensor(exc, incl, tot, ALU.subtract))
                c.link(v.tensor_tensor(off, exc, ps[:, 0, 0:NBE], ALU.add))
                c.link(v.tensor_scalar(off, off, -1.0, None, ALU.add))
                v.tensor_scalar(eq[0], blkf, iota[:, 0:1], None, ALU.is_equal).then_inc(dv_rank[l], 1)
                with loop(dve, 0, NBE // 2) as j:
                    for h in range(2):
                        b = j * 2 + h
                        n = j * 6 + h * 3 + 1
                        dve.wait_ge(dv_rank[l], n)
                        v.tensor_tensor_scan(run[h], ones[:, 0:1].to_broadcast((P, EC)), eq[h], off[:, ds(b, 1)],
                                             ALU.mult, ALU.add).then_inc(dv_rank[l], 1)
                        dve.wait_ge(dv_rank[l], n + 1)
                        v.tensor_scalar(eq[1 - h], blkf, iota[:, ds(b + 1, 1)], None, ALU.is_equal).then_inc(dv_rank[l], 1)
                        v.copy_predicated(rank, eq[h].bitcast(i32), run[h]).then_inc(dv_rank[l], 1)
                dve.wait_ge(dv_rank[l], 3 * NBE + 1)
                v.tensor_copy(posi.bitcast(i32), rank).then_inc(pos_ready, 1)
                c.link(v.tensor_scalar(nwin, tot, float(SW - 1), None, ALU.add))
                c.link(v.tensor_copy(nwi.bitcast(i32), nwin))
                c.link(v.tensor_scalar(nwi.bitcast(i32), nwi.bitcast(i32), SW.bit_length() - 1, None, ALU.arith_shift_right))
                c.link(v.tensor_copy(nwin, nwi.bitcast(i32)))
                c.link(v.tensor_tensor_scan(wend, ones[:, 0:NBE], nwin, 0.0, ALU.mult, ALU.add))
                c.link(v.scalar_tensor_tensor(pad, nwin, float(SW), tot, ALU.mult, ALU.subtract))
                for q in range(Q):
                    i = cst[:, C_WIN + q:C_WIN + q + 1]
                    c.link(v.tensor_scalar(mask[:, 0:NB], wend[:, 0:NB], i, None, ALU.is_le))
                    c.link(v.tensor_reduce(wb_[:, q:q + 1], mask[:, 0:NB], AX.X, ALU.add))
                    c.link(v.tensor_tensor(mask[:, 0:NB], mask[:, 0:NB], pad[:, 0:NB], ALU.mult))
                    c.link(v.tensor_reduce(wpad[:, q:q + 1], mask[:, 0:NB], AX.X, ALU.add))
                c.link(v.scalar_tensor_tensor(wst, cst[:, C_WIN:C_WIN + Q], float(SW), wpad, ALU.mult, ALU.subtract))
                c.link(v.tensor_scalar(wst, wst, float(EN), None, ALU.min))
                c.link(v.tensor_scalar(wb_, wb_, float(NB - 1), None, ALU.min))
                c.link(v.tensor_scalar(wbase, wb_, float(P), None, ALU.mult))
                c.link(v.tensor_copy(wsti, wst))
                c.link(v.tensor_copy(wbi, wb_))
                v.memset(junk[:, 1:2], 0.0).then_inc(tabs_ready, 1)

            dve.wait_ge(in_c, 16)
            ranks(0)
            dve.wait_ge(in_ws, 32)
            c.link(v.tensor_tensor(ws[:, :], ws[:, :], scl, ALU.mult))
            dve.wait_ge(in_x, 16)
            with loop(dve, 0, NB) as b:
                v.bn_stats(stats[:, ds(b, 1), :].rearrange("p b s -> p (b s)"),
                           xs[:, ds(b, 1), :].rearrange("p b s -> p (b s)")).then_inc(dv_bn, 1)
            dve.wait_ge(dv_bn, NB)
            me, mo, ve, vo = (stats[:, :, k:k + 1].rearrange("p b s -> p (b s)") for k in (1, 4, 2, 5))
            c.link(v.tensor_tensor(mean, me, mo, ALU.add))
            c.link(v.tensor_scalar(mean, mean, 0.5, None, ALU.mult))
            c.link(v.tensor_tensor(tmpn, me, mean, ALU.subtract))
            c.link(v.tensor_tensor(tmpn, tmpn, tmpn, ALU.mult))
            c.link(v.tensor_tensor(var, ve, vo, ALU.add))
            c.link(v.tensor_scalar(var, var, 1.0 / F, EPS, ALU.mult, ALU.add))
            v.tensor_tensor(var, var, tmpn, ALU.add).then_inc(var_ready, 1)
            dve.wait_ge(std_ready, 1)
            c.link(v.reciprocal(rstd, tmpn))

            def over(a):
                return a.rearrange("p (b o) -> p b o", o=1).to_broadcast((P, NB, F))

            c.link(v.tensor_tensor(hS[:, :, :], xs, over(mean), ALU.subtract))
            c.link(v.tensor_tensor(hS[:, :, :], hS[:, :, :], over(rstd), ALU.mult))
            v.tensor_scalar(hS[:, :, :], hS[:, :, :], 0.0, None, ALU.max).then_inc(h_ready, 1)
            ranks(1)
            dve.wait_ge(pos_stored, 32)
            dve.wait_ge(tabs_stored, 96)
            dve.wait_ge(tail_stored, 32)
            dve.wait_ge(h_ready, 1)
            c.link(v.memset(acc[:, :], 0.0))
            dve.wait_ge(tab_in, 48)

            def products(it, s):
                dve.wait_ge(row_in[0][s], (it + 1) * 32)
                w = it * SLOTS + s
                dve.wait_ge(key_done[0], w + 1)
                for cc in range(2):
                    v.tensor_scalar(oh[:, s, cc, :], iota, base[:, ds(w, 1)], keyf[:, s, cc:cc + 1],
                                    ALU.add, ALU.is_equal).then_inc(built[0], 1)
                rr = rw0[:, s, :, 2:5].bitcast(f32)
                x0r = xu[:, s, :, 2 * F:2 * F + 3 * S].rearrange("p c (k u) -> p c k u", k=3)
                v.tensor_tensor(x0r, xu[:, s, :, 0:S].rearrange("p c (o u) -> p c o u", o=1).to_broadcast((P, 2, 3, S)),
                                rr.rearrange("p c (k o) -> p c k o", o=1).to_broadcast((P, 2, 3, S)), ALU.mult).then_inc(built[0], 1)
                x1r = xu[:, s, :, 2 * F + 3 * S:A0].rearrange("p c (u k) -> p c u k", k=3)
                v.tensor_tensor(x1r, xu[:, s, :, S:F].rearrange("p c (u k) -> p c u k", k=3),
                                rr.rearrange("p c (o k) -> p c o k", o=1).to_broadcast((P, 2, V, 3)), ALU.mult).then_inc(built[0], 1)

            def add(l, w, s, first):
                blk = dve.value_load(tab[0:1, ds(w + W, 1)], min_val=0, max_val=NB - 1)
                dve.wait_ge(summed[l], w + 1)
                if not first:
                    dve.wait_ge(added[l], w)
                if l == 0:
                    a = acc[:, ds(blk * A0, A0)].rearrange("p (j f) -> p j f", j=2)
                    t = ps[:, 2 * (s % 2):2 * (s % 2) + 2, 0:HALF]
                else:
                    a, t = acc1[:, ds(blk * F, F)], ps[:, s % 2, 0:F]
                v.tensor_tensor(a, a, t, ALU.add).then_inc(added[l], 1)

            for s in range(SLOTS):
                products(0, s)
                if s:
                    add(0, s - 1, s - 1, s == 1)
            with loop(dve, 1, W // SLOTS) as it:
                for s in range(SLOTS):
                    products(it, s)
                    add(0, it * SLOTS + s - 1, (s - 1) % SLOTS, False)
            add(0, W - 1, SLOTS - 1, False)
            dve.wait_ge(added[0], W)

            U_DVE = 28

            def node(b, first):
                n = Steps(u_dve, b * U_DVE)
                h = hS[:, ds(b, 1), :].rearrange("p b f -> p (b f)")
                x1 = hS[:, ds(b, 1), S:F].rearrange("p b (u k) -> p (b u) k", k=3)
                a1 = aS[:, S:F].rearrange("p (u k) -> p u k", k=3)
                dve.wait_ge(agg_sb, b + 1)
                if not first:
                    dve.wait_ge(u_t_out, b * 16)
                gv, g2v = (t.rearrange("p (u w) -> p u w", u=V) for t in (g, g2))
                for k in range(3):
                    n.link(v.tensor_tensor((gv, g2v, g2v)[k], x1[:, :, k:k + 1].to_broadcast((P, V, V)),
                                           a1[:, :, k:k + 1].rearrange("p u o -> p o u").to_broadcast((P, V, V)), ALU.mult))
                    if k:
                        n.link(v.tensor_tensor(g, g, g2, ALU.add))
                v.memset(mv[:, 3:4], 0.0).then_inc(g_done, 1)
                for half, cf in ((0, a1), (1, x1)):
                    dve.wait_ge(z1_mm, b * 2 + half + 1)
                    z = ps[:, 3:5, :].rearrange("p a (j w) -> p (a j) w", w=V)
                    for k in range(3):
                        n.link(v.tensor_tensor(prod.rearrange("p (j w) -> p j w", w=V), z,
                                               cf[:, :, k:k + 1].to_broadcast((P, V, V)), ALU.mult))
                        r = v.tensor_reduce(o1[:, (half * 3 + k) * V:(half * 3 + k + 1) * V],
                                            prod.rearrange("p (j w) -> p w j", w=V), AX.X, ALU.add)
                        n.link(r)
                    v.memset(mv[:, 3:4], 0.0).then_inc(z1_used, 1)
                for j in range(8):
                    dve.wait_ge(z0_mm, b * 8 + j + 1)
                    if j >= 2:
                        dve.wait_ge(z0_sum, b * 8 + j - 1)
                    pj = prod[:, 512 * (j % 2):512 * (j % 2) + 512]
                    v.tensor_tensor(pj.rearrange("p (u w) -> p u w", w=S),
                                    ps[:, j % 2, :].rearrange("p (u w) -> p u w", w=S),
                                    cat[:, S + 8 * j:S + 8 * j + 8].rearrange("p (u o) -> p u o", o=1).to_broadcast((P, 8, S)),
                                    ALU.mult).then_inc(z0_prod, 1)
                dve.wait_ge(z0_sum, b * 8 + 8)
                n.link(v.tensor_reduce(prod[:, 0:S], ps[:, 2, :].rearrange("p (u w) -> p w u", w=S), AX.X, ALU.add))
                n.link(v.tensor_tensor(o1[:, 0:3 * V], o1[:, 0:3 * V], o1[:, 3 * V:6 * V], ALU.add))
                po = ps[:, 7, 256:256 + F]
                dve.wait_ge(out_mm, b + 1)
                if not first:
                    dve.wait_ge(u_x2_out, b * 16)
                n.link(v.scalar_tensor_tensor(y[:, 0:S], prod[:, 0:S], 5120.0 ** -0.5, po[:, 0:S], ALU.mult, ALU.add))
                n.link(v.scalar_tensor_tensor(y[:, S:F].rearrange("p (w k) -> p k w", k=3),
                                              o1[:, 0:3 * V].rearrange("p (k w) -> p k w", k=3), 1.0 / 64,
                                              po[:, S:F].rearrange("p (w k) -> p k w", k=3), ALU.mult, ALU.add))
                n.link(v.tensor_tensor(y, y, h, ALU.add))
                dve.wait_ge(u_x_in, (b + 1) * 16)
                n.link(v.tensor_tensor(y, y, xb, ALU.add))
                v.memset(mv[:, 3:4], 0.0).then_inc(y_done, 1)
                n.link(v.bn_stats(st6, y))
                v.memset(mv[:, 3:4], 0.0)
                n.link(v.bn_aggr(mv[:, 0:2], st6))
                v.tensor_scalar(mv[:, 2:3], mv[:, 1:2], EPS, None, ALU.add).then_inc(u_var, 1)
                dve.wait_ge(u_std, b + 1)
                n.link(v.reciprocal(mv[:, 3:4], mv[:, 2:3]))
                n.link(v.tensor_scalar(hb, y, mv[:, 0:1], mv[:, 3:4], ALU.subtract, ALU.mult))
                v.tensor_scalar(hb, hb, 0.0, None, ALU.max).then_inc(h2_done, 1)
                assert n.n == U_DVE - 1, n.n
                n.link(v.memset(mv[:, 1:2], 0.0))

            node(0, True)
            with loop(dve, 1, NB) as b:
                node(b, False)

            dve.wait_ge(tab_in, 96)
            dve.wait_ge(h2_kept, NB)
            c.link(v.memset(acc1, 0.0))

            def messages(it, s, first):
                w = it * SLOTS + s
                t2 = s % 2
                dve.wait_ge(key_done[1], w + 1)
                if not first:
                    dve.wait_ge(summed[1], w - 1)
                for cc in range(2):
                    v.tensor_scalar(oh1[:, t2, cc, :], iota, base[:, ds(w, 1)], keyf[:, s, cc:cc + 1],
                                    ALU.add, ALU.is_equal).then_inc(built[1], 1)
                dve.wait_ge(row_in[1][s], (it + 1) * 32)
                dve.wait_ge(scaled[1], (w + 1) * 2)
                n0 = w * 10
                ev = [[rw1[:, s, cc * R1 + 3 + d:cc * R1 + 4 + d].bitcast(f32) for d in range(3)] for cc in range(2)]
                for k, (d, o, n, t) in enumerate(((0, 0, S + V, F + S), (1, V, S + V, F), (2, V, S, F + 160), (2, S + 2 * V, V, F + S))):
                    for cc in range(2):
                        if k in (1, 2):
                            dve.wait_ge(built[1], n0 + 2 + 2 * (k - 1) + cc + 1)
                        m = mg[:, t2, cc, o:o + n]
                        v.scalar_tensor_tensor(m, tb[:, s, cc, t:t + n], ev[cc][d], m, ALU.mult, ALU.add).then_inc(built[1], 1)
                dve.wait_ge(gate_done, w + 1)
                dve.wait_ge(built[1], n0 + 10)
                m = mg[:, t2, :, :].rearrange("p c f -> p (c f)")
                v.tensor_tensor(m, m, gt[:, t2, :], ALU.mult).then_inc(msg, 1)

            for s in range(SLOTS):
                messages(0, s, s < 2)
                if s:
                    add(1, s - 1, s - 1, s == 1)
            with loop(dve, 1, W // SLOTS) as it:
                for s in range(SLOTS):
                    messages(it, s, False)
                    add(1, it * SLOTS + s - 1, (s - 1) % SLOTS, False)
            add(1, W - 1, SLOTS - 1, False)
            dve.wait_ge(added[1], W)

            def last(b, first):
                n = Steps(f_dve, b * 4)
                if not first:
                    dve.wait_ge(f_pe, (b - 1) * 2 + 1)
                a = acc1[:, ds(b * F, F)]
                h = hS[:, ds(b, 1), :].rearrange("p b f -> p (b f)")
                hv = hS[:, ds(b, 1), S:F].rearrange("p b (u k) -> p (b k) u", k=3)
                n.inc(v.tensor_tensor(fh[:, V:V + S], a[:, V:V + S], h[:, 0:S], ALU.add))
                n.inc(v.tensor_tensor(fh[:, 0:V], a[:, 0:V], hv[:, 0, :], ALU.add))
                n.inc(v.tensor_tensor(fh[:, S + V:F].rearrange("p (k u) -> p k u", u=V),
                                      a[:, S + V:F].rearrange("p (k u) -> p k u", u=V), hv[:, 1:3, :], ALU.add))
                dve.wait_ge(f_x_in, (b + 1) * 16)
                dve.wait_ge(f_pe, b * 2 + 2)
                if not first:
                    dve.wait_ge(f_out, b * 16)
                n.inc(v.tensor_tensor(fo, ps[:, 7, 0:F], fx, ALU.add))

            last(0, True)
            with loop(dve, 1, NB) as b:
                last(b, False)

        @block.scalar
        def _(act):
            a = nc.scalar
            act.wait_ge(var_ready, 1)
            a.activation(tmpn, var, ACT.Sqrt).then_inc(std_ready, 1)

            def dist(it, s, first):
                w = it * SLOTS + s
                act.wait_ge(rec_in[0][s], (it + 1) * 16)
                if not first:
                    act.wait_ge(built[0], (w - SLOTS + 1) * 4)
                a.activation(keyf[:, s, :], rw0[:, s, :, 1:2].rearrange("p c o -> p (c o)"), ACT.Copy).then_inc(key_done[0], 1)
                act.wait_ge(row_in[0][s], (it + 1) * 32)
                for cc in range(2):
                    a.activation(xu[:, s, cc, F:2 * F], xu[:, s, cc, 0:F], ACT.Copy,
                                 scale=rw0[:, s, cc, 5:6].bitcast(f32)).then_inc(scaled[0], 1)

            for s in range(SLOTS):
                dist(0, s, True)
            with loop(act, 1, W // SLOTS) as it:
                for s in range(SLOTS):
                    dist(it, s, False)

            def node(b, first):
                h = hS[:, ds(b, 1), :].rearrange("p b f -> p (b f)")
                if not first:
                    act.wait_ge(h2_kept, b)
                a.activation(ab, acc[:, ds(b * A0, A0)], ACT.Copy)
                a.activation(hb, h, ACT.Copy).then_inc(agg_c, 1)
                act.wait_ge(agg_t, b + 1)
                a.activation(aT[:, 0:4 * P], ps[:, 5, :], ACT.Copy)
                a.activation(aT[0:A0 - 4 * P, 4 * P:5 * P], ps[0:A0 - 4 * P, 6, 0:P], ACT.Copy).then_inc(agg_t_sb, 1)
                act.wait_ge(agg_mm, b + 1)
                a.activation(aS, ps[:, 7, 0:F], ACT.Copy)
                a.activation(cat[:, 0:S], ps[:, 7, 0:S], ACT.Copy)
                a.activation(cat[:, S:P], h[:, 0:S], ACT.Copy).then_inc(agg_sb, 1)
                act.wait_ge(h_t, b + 1)
                a.activation(catT, ps[:, 5, 0:P], ACT.Copy)
                a.activation(hT[:, 0:P], ps[:, 5, P:2 * P], ACT.Copy)
                a.activation(hT[0:V, P:2 * P], ps[0:V, 5, 2 * P:3 * P], ACT.Copy).then_inc(h_t_sb, 1)
                act.wait_ge(g_t, b + 1)
                a.activation(gT, ps[:, 5:7, :].rearrange("p a f -> p (a f)"), ACT.Copy).then_inc(g_t_sb, 1)
                act.wait_ge(u_var, b + 1)
                a.activation(mv[:, 2:3], mv[:, 2:3], ACT.Sqrt).then_inc(u_std, 1)
                act.wait_ge(h2_t, b + 1)
                a.activation(hT[:, 0:P], ps[:, 5, 0:P], ACT.Copy)
                a.activation(hT[0:V, P:2 * P], ps[0:V, 5, P:2 * P], ACT.Copy).then_inc(h2_t_sb, 1)
                a.activation(h, hb, ACT.Copy).then_inc(h2_kept, 1)
                act.wait_ge(t_mm, b + 1)
                a.activation(tS, ps[:, 6, 0:TW], ACT.Copy).then_inc(t_sb, 1)

            act.wait_ge(added[0], W)
            node(0, True)
            with loop(act, 1, NB) as b:
                node(b, False)

            def gates(it, s, first):
                w = it * SLOTS + s
                t2 = s % 2
                act.wait_ge(rec_in[1][s], (it + 1) * 16)
                if not (first and s < SLOTS):
                    act.wait_ge(msg, w - SLOTS + 1)
                a.activation(keyf[:, s, :], rw1[:, s, :].rearrange("p (c r) -> p c r", c=2)[:, :, 1:2].rearrange("p c o -> p (c o)"),
                             ACT.Copy).then_inc(key_done[1], 1)
                act.wait_ge(attr_t, w + 1)
                if not (first and s < 2):
                    act.wait_ge(gate_mm, w - 1)
                a.activation(atr[0:2 * R1, t2, :], ps[0:2 * R1, 4 + t2, 0:P], ACT.Copy).then_inc(attr_c, 1)
                if not (first and s < 2):
                    act.wait_ge(msg, w - 1)
                act.wait_ge(gate_mm, w + 1)
                a.activation(gt[:, t2, :].rearrange("p (c f) -> p c f", c=2), ps[:, 2 + 4 * t2:4 + 4 * t2, 0:F], ACT.Sigmoid).then_inc(gate_done, 1)
                if not (first and s < 2):
                    act.wait_ge(summed[1], w - 1)
                act.wait_ge(row_in[1][s], (it + 1) * 32)
                for cc in range(2):
                    a.activation(mg[:, t2, cc, :], tb[:, s, cc, 0:F], ACT.Copy,
                                 scale=rw1[:, s, cc * R1 + 2:cc * R1 + 3].bitcast(f32)).then_inc(scaled[1], 1)

            for s in range(SLOTS):
                gates(0, s, True)
            with loop(act, 1, W // SLOTS) as it:
                for s in range(SLOTS):
                    gates(it, s, False)

            with loop(act, 0, NB) as b:
                act.wait_ge(f_pe, b * 2 + 1)
                a.activation(fT[:, 0:P], ps[:, 5, 0:P], ACT.Copy)
                a.activation(fT[0:V, P:2 * P], ps[0:V, 5, P:2 * P], ACT.Copy).then_inc(f_act, 1)

        @block.tensor
        def _(pe):
            t = nc.tensor

            def flip(dst, src):
                return t.matmul(dst, src, ident, start=True, stop=True)

            pe.wait_ge(in_c, 16)
            for l in range(2):
                pe.wait_ge(cnt_ready, l + 1)
                t.matmul(ps[:, 0, 0:NBE], tri, cnt, start=True, stop=True)
                t.matmul(ps[:, 0, 64:64 + NBE], ones, cnt, start=True, stop=True).then_inc(off_ready, 1)

            def sums(it, s, first):
                w = it * SLOTS + s
                pe.wait_ge(built[0], (w + 1) * 4)
                pe.wait_ge(scaled[0], (w + 1) * 2)
                if not (first and s < 2):
                    pe.wait_ge(added[0], w - 1)
                for cc in range(2):
                    for j in range(2):
                        last = t.matmul(ps[:, 2 * (s % 2) + j, 0:HALF], oh[:, s, cc, :],
                                        xu[:, s, cc, j * HALF:(j + 1) * HALF], start=(cc == 0), stop=(cc == 1))
                last.then_inc(summed[0], 1)

            for s in range(SLOTS):
                sums(0, s, True)
            with loop(pe, 1, W // SLOTS) as it:
                for s in range(SLOTS):
                    sums(it, s, False)

            pe.wait_ge(added[0], W)
            pe.wait_ge(wbig_in, 16)

            def node(b, first):
                pe.wait_ge(agg_c, b + 1)
                if not first:
                    pe.wait_ge(t_sb, b)
                for k in range(KC):
                    n = min(P, A0 - k * P)
                    last = flip(ps[0:n, 5 + k // 4, (k % 4) * P:(k % 4) * P + P], ab[:, k * P:k * P + n])
                last.then_inc(agg_t, 1)
                pe.wait_ge(agg_t_sb, b + 1)
                for k in range(KC):
                    n = min(P, A0 - k * P)
                    last = t.matmul(ps[:, 7, 0:F], aT[0:n, k * P:(k + 1) * P], ws[0:n, WB + k * F:WB + (k + 1) * F],
                                    start=(k == 0), stop=(k == KC - 1))
                last.then_inc(agg_mm, 1)
                pe.wait_ge(agg_sb, b + 1)
                flip(ps[:, 5, 0:P], cat)
                flip(ps[:, 5, P:2 * P], hb[:, 0:P])
                flip(ps[0:V, 5, 2 * P:3 * P], hb[:, P:F]).then_inc(h_t, 1)
                pe.wait_ge(h_t_sb, b + 1)
                for half, lo in ((0, S), (1, 0)):
                    if half:
                        pe.wait_ge(z1_used, b * 2 + 1)
                    for j in range(2):
                        last = t.matmul(ps[:, 3 + j, :], catT[lo:lo + S, :], w1x1[lo:lo + S, j * 512:(j + 1) * 512],
                                        start=True, stop=True)
                    last.then_inc(z1_mm, 1)
                for j in range(9):
                    if j < 8:
                        if j >= 2:
                            pe.wait_ge(z0_prod, b * 8 + j - 1)
                        t.matmul(ps[:, j % 2, :], catT[0:S, :], w000[0:S, j * 512:(j + 1) * 512],
                                 start=True, stop=True).then_inc(z0_mm, 1)
                    if j:
                        pe.wait_ge(z0_prod, b * 8 + j)
                        t.matmul(ps[:, 2, :], ident, prod[:, 512 * ((j - 1) % 2):512 * ((j - 1) % 2) + 512],
                                 start=(j == 1), stop=(j == 8)).then_inc(z0_sum, 1)
                    if j == 0:
                        pe.wait_ge(g_done, b + 1)
                        for k in range(8):
                            last = flip(ps[:, 5 + k // 4, (k % 4) * P:(k % 4) * P + P], g[:, k * P:(k + 1) * P])
                        last.then_inc(g_t, 1)
                t.matmul(ps[:, 7, 256 + S:256 + F], hT[:, 0:P], ws[:, WU + S:WU + F], start=True, stop=False)
                t.matmul(ps[:, 7, 256 + S:256 + F], hT[0:V, P:2 * P], ws[0:V, WU + F + S:WU + 2 * F], start=False, stop=True)
                t.matmul(ps[:, 7, 256:256 + S], hT[:, 0:P], ws[:, WU:WU + S], start=True, stop=False)
                t.matmul(ps[:, 7, 256:256 + S], hT[0:V, P:2 * P], ws[0:V, WU + F:WU + F + S], start=False, stop=False)
                pe.wait_ge(g_t_sb, b + 1)
                for k in range(8):
                    last = t.matmul(ps[:, 7, 256:256 + S], gT[:, k * P:(k + 1) * P], ws[:, W110 + k * S:W110 + (k + 1) * S],
                                    start=False, stop=(k == 7))
                last.then_inc(out_mm, 1)
                pe.wait_ge(h2_done, b + 1)
                flip(ps[:, 5, 0:P], hb[:, 0:P])
                flip(ps[0:V, 5, P:2 * P], hb[:, P:F]).then_inc(h2_t, 1)
                pe.wait_ge(h2_t_sb, b + 1)
                t.matmul(ps[:, 6, 0:TW], hT[:, 0:P], ws[:, WT:WT + TW], start=True, stop=False)
                t.matmul(ps[:, 6, 0:TW], hT[0:V, P:2 * P], ws[0:V, WT + TW:WT + 2 * TW], start=False, stop=True).then_inc(t_mm, 1)

            node(0, True)
            with loop(pe, 1, NB) as b:
                node(b, False)

            def gate(it, s, first):
                w = it * SLOTS + s
                t2 = s % 2
                pe.wait_ge(rec_in[1][s], (it + 1) * 16)
                if not (first and s < 2):
                    pe.wait_ge(attr_c, w - 1)
                flip(ps[0:2 * R1, 4 + t2, 0:P], rw1[:, s, :].bitcast(f32)).then_inc(attr_t, 1)
                pe.wait_ge(attr_c, w + 1)
                if not (first and s < 2):
                    pe.wait_ge(gate_done, w - 1)
                for cc in range(2):
                    k = slice(cc * R1, (cc + 1) * R1)
                    last = t.matmul(ps[:, 2 + 4 * t2 + cc, 0:F], atr[k, t2, :], ws[k, WG:WG + F], start=True, stop=True)
                last.then_inc(gate_mm, 1)

            def sums1(w, s, first):
                pe.wait_ge(msg, w + 1)
                if not (first and s < 2):
                    pe.wait_ge(added[1], w - 1)
                for cc in range(2):
                    last = t.matmul(ps[:, s % 2, 0:F], oh1[:, s % 2, cc, :], mg[:, s % 2, cc, :],
                                    start=(cc == 0), stop=(cc == 1))
                last.then_inc(summed[1], 1)

            pe.wait_ge(t_sb, NB)
            for s in range(SLOTS):
                gate(0, s, True)
                if s:
                    sums1(s - 1, s - 1, True)
            with loop(pe, 1, W // SLOTS) as it:
                for s in range(SLOTS):
                    gate(it, s, False)
                    sums1(it * SLOTS + s - 1, (s - 1) % SLOTS, False)
            sums1(W - 1, SLOTS - 1, False)

            def last_block(b, first):
                pe.wait_ge(f_dve, b * 4 + 3)
                if not first:
                    pe.wait_ge(f_act, b)
                flip(ps[:, 5, 0:P], fh[:, 0:P])
                flip(ps[0:V, 5, P:2 * P], fh[:, P:F]).then_inc(f_pe, 1)
                pe.wait_ge(f_act, b + 1)
                t.matmul(ps[:, 7, 0:F], fT[:, 0:P], ws[:, WF:WF + F], start=True, stop=False)
                t.matmul(ps[:, 7, 0:F], fT[0:V, P:2 * P], ws[0:V, WF + F:WF + 2 * F], start=False, stop=True).then_inc(f_pe, 1)

            pe.wait_ge(gate_done, W)
            last_block(0, True)
            with loop(pe, 1, NB) as b:
                last_block(b, False)


_ORDER = ["x", "rec0", "rec1", "key0", "key1", "wsmall", "wscale", "wbig", "const"]


def constants():
    c = np.zeros((P, CW), np.float32)
    c[:, C_ID:C_ID + P] = np.eye(P)
    c[:, C_TRI:C_TRI + P] = np.triu(np.ones((P, P)), 1)
    c[:, C_ONE:C_ONE + P] = 1.0
    c[:, C_IOTA:C_IOTA + P] = np.arange(P)
    c[:, C_WIN:C_WIN + Q] = np.arange(Q * P).reshape(Q, P).T
    return c


def place(ws, w000, w011, w101, w110, lm0, lm1, m000, m011, m101, m110, lu0, lu1, ss, sv, vs, vv, rad, bias, ls, lv):
    full = np.zeros((KC * P, F), np.float32)
    full[0:S, 0:S] = lm0
    full[F:F + S, 0:S] = m000
    for k in range(3):
        full[S + k:F:3, S + k::3] = lm1
        full[F + S + k:2 * F:3, S + k::3] = m101
        full[2 * F + k * S:2 * F + (k + 1) * S, S + k::3] = m011
        full[2 * F + 3 * S + k:A0:3, 0:S] = m110
    for k in range(KC):
        ws[:, WB + k * F:WB + (k + 1) * F] = full[k * P:(k + 1) * P]

    def two(at, m, n):
        ws[:, at:at + n] = m[0:P]
        ws[0:V, at + n:at + 2 * n] = m[P:F]

    t = np.zeros((F, TW), np.float32)
    t[0:S, V:V + S] = ss
    t[0:S, F + S:F + S + V] = sv
    for k in range(3):
        at = (0, S + V, S + 2 * V)[k]
        t[S + k::3, at:at + V] = vs
        at = (F + S + V, F, F + 160)[k]
        t[S + k::3, at:at + S] = vv
    two(WT, t, TW)
    u = np.zeros((F, F), np.float32)
    u[0:S, 0:S] = lu0
    f = np.zeros((F, F), np.float32)
    f[V:V + S, 0:S] = ls
    for k in range(3):
        u[S + k::3, S + k::3] = lu1
        at = (0, S + V, S + 2 * V)[k]
        f[at:at + V, S + k::3] = lv
    two(WU, u, F)
    two(WF, f, F)
    order = [*range(S, F, 3), *range(S), *range(S + 1, F, 3), *range(S + 2, F, 3)]
    for c in range(2):
        ws[c * R1 + 6:c * R1 + 22, WG:WG + F] = rad[order].T
        ws[c * R1 + 22, WG:WG + F] = bias[order]
    for c in range(8):
        ws[:, W110 + c * S:W110 + (c + 1) * S] = w110[c * P:(c + 1) * P]


def kernel(**inputs):
    import numpy as _np
    import concourse.bacc as _bacc
    from concourse import mybir as _mybir
    from concourse.bass_utils import run_bass_kernel_spmd as _run

    g = {k: _np.asarray(a) for k, a in inputs.items()}
    one = lambda shape, value: _np.full(shape, value, _np.float32)
    x = _np.zeros((NN, F), _np.float32)
    x[0:N] = g["x"]
    src = _np.full((EN,), NN - 1, _np.int32)
    dst = _np.full((EN,), NN - 1, _np.int32)
    src[0:E], dst[0:E] = g["src"], g["dst"]
    rec1 = _np.zeros((EN, R1), _np.int32)
    rec1[:, 0], rec1[:, 1] = src, dst
    rec1[0:E, 2:6] = g["edge_attr_4"].view(_np.int32)
    rec1[0:E, 6:22] = g["edge_attr_16"].view(_np.int32)
    rec1[:, 22] = _np.ones((EN,), _np.float32).view(_np.int32)
    rec0 = _np.zeros((EN, R0), _np.int32)
    rec0[:, 0], rec0[:, 1] = dst, src
    rec0[0:E, 2:6] = g["edge_attr_4"].view(_np.int32)
    p0, p1 = "L0_gnn_", "L1_gnn_"
    wsmall, wscale = _np.zeros((P, WS), _np.float32), _np.zeros((P, WS), _np.float32)
    r2, r3 = 2.0 ** -0.5, 3.0 ** -0.5
    place(wsmall, None, None, None, g[p0 + "wu110"].reshape(V * V, S), g[p0 + "lm0"], g[p0 + "lm1"],
          g[p0 + "wm000"][:, 0], g[p0 + "wm011"][:, 0], g[p0 + "wm101"][:, 0], g[p0 + "wm110"][:, 0],
          g[p0 + "lu0"], g[p0 + "lu1"], g[p1 + "W_ss"], g[p1 + "W_sv"], g[p1 + "W_vs"], g[p1 + "W_vv"],
          g[p1 + "W_rad"], g[p1 + "b_rad"], g[p1 + "L_s"], g[p1 + "L_v"])
    m = (S + V) ** -0.5
    place(wscale, None, None, None, one((V * V, S), r3 * 5120.0 ** -0.5), S ** -0.5, V ** -0.5, m, m, m, m * r3,
          S ** -0.5, V ** -0.5, r2 * S ** -0.5, r2 * r3 * S ** -0.5, r2 * r3 * V ** -0.5, r2 * r3 * V ** -0.5,
          one((F, 16), 1.0), one((F,), 1.0), S ** -0.5, V ** -0.5)
    wbig = _np.zeros((P, S * S + V * V), _np.float32)
    wbig[0:S, 0:S * S] = g[p0 + "wu000"].transpose(1, 0, 2).reshape(S, S * S)
    wbig[0:S, S * S:] = g[p0 + "wu101"].transpose(1, 0, 2).reshape(S, V * V)
    wbig[S:P, S * S:] = g[p0 + "wu011"].reshape(S, V * V)
    arrays = {"x": x, "rec0": rec0.reshape(P, EC * R0), "rec1": rec1.reshape(P, EC * R1), "key0": src.reshape(P, EC),
              "key1": dst.reshape(P, EC), "wsmall": wsmall, "wscale": wscale, "wbig": wbig, "const": constants()}
    nc = _bacc.Bacc("TRN2", target_bir_lowering=False, num_devices=1)
    args = [nc.dram_tensor(f"in_{n}", arrays[n].shape, _mybir.dt.from_np(arrays[n].dtype), kind="ExternalInput").ap()
            for n in _ORDER]
    o = nc.dram_tensor("out_0", (NN, F), _mybir.dt.float32, kind="ExternalOutput").ap()
    program(nc, *args, o)
    r = _run(nc, [{f"in_{n}": arrays[n] for n in _ORDER}], core_ids=[0])
    return r.results[0]["out_0"][0:N]
```

```python
from contextlib import ExitStack

import concourse.bass as bass
from concourse import mybir
import numpy as np

P = 128
N, E = 6250, 100000
F, S, V = 160, 64, 32
NB = -(-N // P)
NBE = NB + NB % 2
NN = NB * P
EC = -(-E // P)
EN = EC * P
SW = 2 * P
SLOTS = 4
W = (EN + NB * (SW - 1)) // SW
W = -(-W // SLOTS) * SLOTS
Q = -(-W // P)
R0, R1 = 8, 32
CH = 17
PIECES = EC // CH
assert PIECES * CH == EC and PIECES % 2 == 0
A0 = F + F + 3 * S + 3 * V
HALF = A0 // 2
TW = 384
KC = -(-A0 // P)
WB, WT, WU, WF, WG, W110 = 0, KC * F, KC * F + 2 * TW, KC * F + 2 * TW + F, KC * F + 2 * TW + 3 * F, KC * F + 2 * TW + 4 * F
WS = W110 + 8 * S
C_ID, C_TRI, C_ONE, C_IOTA, C_WIN = 0, P, 2 * P, 3 * P, 4 * P
CW = 4 * P + Q
EPS = 1e-5


def program(nc, xin, rec0, rec1, key0, key1, wsmall, wscale, wbig, const, out):
    f32, i32 = mybir.dt.float32, mybir.dt.int32
    ALU, ACT, AX = mybir.AluOpType, mybir.ActivationFunctionType, mybir.AxisListType
    ds = bass.ds
    ctx = ExitStack()
    with ctx:
        ctx.enter_context(nc.allow_non_contiguous_dma(reason="short tables"))

        def sb(name, shape, dt=f32):
            return ctx.enter_context(nc.sbuf_tensor(name, shape, dt))

        def sem(name):
            return ctx.enter_context(nc.semaphore(name))

        hD = nc.dram_tensor("h_rows", [NN, F], f32).ap()
        tD = nc.dram_tensor("t_rows", [NN, TW], f32).ap()
        x2D = nc.dram_tensor("x2_rows", [NN, F], f32).ap()
        posD = [nc.dram_tensor(f"pos{l}", [P, EC], i32).ap() for l in range(2)]
        eD = [nc.dram_tensor(f"sorted{l}", [EN + SW, r], i32).ap() for l, r in ((0, R0), (1, R1))]
        tabD = [nc.dram_tensor(f"windows{l}", [2, Q * P], i32).ap() for l in range(2)]
        baseD = [nc.dram_tensor(f"bases{l}", [1, Q * P], f32).ap() for l in range(2)]

        acc = sb("acc", [P, NB * A0])
        acc1 = acc[:, 0:NB * F]
        hS = sb("hS", [P, NB, F])
        RW = 9552
        room = sb("room", [P, RW])
        ws = sb("ws", [P, WS])
        cst = sb("cst", [P, CW])
        base = sb("base", [P, W])
        tab = sb("tab", [1, 2 * W], i32)
        rw0 = sb("rw0", [P, SLOTS, 2, R0], i32)
        rw1 = sb("rw1", [P, SLOTS, 2 * R1], i32)
        srec = sb("srec", [P, 2, CH * R1], i32)
        spos = sb("spos", [P, 2, CH], i32)
        keyf = sb("keyf", [P, SLOTS, 2])
        ps = ctx.enter_context(nc.psum_tensor("ps", [P, 8, 512], f32))

        ident, tri, ones, iota = (cst[:, c:c + P] for c in (C_ID, C_TRI, C_ONE, C_IOTA))

        at = [0]

        def early(words):
            at[0] += words
            return acc[:, at[0] - words:at[0]]

        keys, blki, blkf, rank, posi = (early(EC) for _ in range(5))
        eq = [early(EC) for _ in range(2)]
        run = [early(EC) for _ in range(2)]
        scl = early(WS)
        xs = early(NB * F).rearrange("p (b f) -> p b f", f=F)
        tail = early(2 * R1).bitcast(i32)
        cnt, off, tot, incl, exc, nwin, nwi, wend, pad, mask, junk = (early(NBE) for _ in range(11))
        stats = early(NB * 6).rearrange("p (b s) -> p b s", s=6)
        mean, var, tmpn, rstd = (early(NB) for _ in range(4))
        wb_, wst, wpad, wbase = (early(Q) for _ in range(4))
        wsti, wbi = (early(Q).bitcast(i32) for _ in range(2))
        assert at[0] <= NB * A0

        in_key = [sem(f"in_key{l}") for l in range(2)]
        in_x, in_c, in_ws = sem("in_x"), sem("in_c"), sem("in_ws")
        cnt_ready, off_ready = sem("cnt_ready"), sem("off_ready")
        pos_ready, pos_stored = sem("pos_ready"), sem("pos_stored")
        tabs_ready, tabs_stored = sem("tabs_ready"), sem("tabs_stored")
        tail_ready, tail_stored = sem("tail_ready"), sem("tail_stored")
        var_ready, std_ready = sem("var_ready"), sem("std_ready")
        h_ready, h_stored = sem("h_ready"), sem("h_stored")
        acc_clear = sem("acc_clear")
        dv = sem("dv")
        dv_cnt = [sem(f"dv_cnt{l}") for l in range(2)]
        dv_rank = [sem(f"dv_rank{l}") for l in range(2)]
        dv_bn = sem("dv_bn")
        piece = [[sem(f"piece{l}{h}") for h in range(2)] for l in range(2)]
        sent = [[sem(f"sent{l}{h}") for h in range(2)] for l in range(2)]
        tab_in = sem("tab_in")
        pool_go = sem("pool_go")
        rec_in = [[sem(f"rec_in{l}{s}") for s in range(SLOTS)] for l in range(2)]
        row_in = [[sem(f"row_in{l}{s}") for s in range(SLOTS)] for l in range(2)]
        key_done = [sem(f"key_done{l}") for l in range(2)]
        scaled = [sem(f"scaled{l}") for l in range(2)]
        built = [sem(f"built{l}") for l in range(2)]
        summed = [sem(f"summed{l}") for l in range(2)]
        added = [sem(f"added{l}") for l in range(2)]
        attr_t, attr_c, gate_mm, gate_done = sem("attr_t"), sem("attr_c"), sem("gate_mm"), sem("gate_done")
        msg = sem("msg")
        wbig_in, u_x_in = sem("wbig_in"), sem("u_x_in")
        agg_c, agg_t, agg_t_sb, agg_mm, agg_sb = sem("agg_c"), sem("agg_t"), sem("agg_t_sb"), sem("agg_mm"), sem("agg_sb")
        h_t, h_t_sb, z1_mm, z1_used = sem("h_t"), sem("h_t_sb"), sem("z1_mm"), sem("z1_used")
        u_norm = sem("u_norm")
        z0_mm, z0_prod, z0_sum = sem("z0_mm"), sem("z0_prod"), sem("z0_sum")
        g_done, g_t, g_t_sb, out_mm = sem("g_done"), sem("g_t"), sem("g_t_sb"), sem("out_mm")
        y_done, u_var, u_std, h2_done = sem("y_done"), sem("u_var"), sem("u_std"), sem("h2_done")
        h2_kept, h2_t, h2_t_sb, t_mm, t_sb = sem("h2_kept"), sem("h2_t"), sem("h2_t_sb"), sem("t_mm"), sem("t_sb")
        u_dve = sem("u_dve")
        u_t_out, u_x2_out = sem("u_t_out"), sem("u_x2_out")
        f_x_in, f_pe, f_act, f_dve, f_out = sem("f_x_in"), sem("f_pe"), sem("f_act"), sem("f_dve"), sem("f_out")

        xu = room[:, 0:SLOTS * 2 * A0].rearrange("p (s c f) -> p s c f", s=SLOTS, c=2)
        oh = room[:, SLOTS * 2 * A0:SLOTS * 2 * (A0 + P)].rearrange("p (s c f) -> p s c f", s=SLOTS, c=2)
        at[0] = 0

        def part(words):
            at[0] += words
            assert at[0] <= RW
            return room[:, at[0] - words:at[0]]

        tb = part(SLOTS * 2 * TW).rearrange("p (s c f) -> p s c f", s=SLOTS, c=2)
        oh1 = part(2 * 2 * P).rearrange("p (s c f) -> p s c f", s=2, c=2)
        mg = part(2 * 2 * F).rearrange("p (s c f) -> p s c f", s=2, c=2)
        gt = part(2 * 2 * F).rearrange("p (s f) -> p s f", s=2)
        atr = part(2 * P).rearrange("p (s f) -> p s f", s=2)
        at[0] = 0
        w000 = part(S * S // 2)
        w1x1 = part(V * V)
        mb = part(3 * 512)
        pz = part(2 * 512)
        g = part(1024)
        aT = part(KC * P)
        ab = aT[:, 0:A0]
        cat = part(3 * S)
        aS = [part(F) for _ in range(2)]
        catT = [part(P) for _ in range(2)]
        catU = [part(P) for _ in range(2)]
        x1T = [part(P) for _ in range(2)]
        x1b, hb = part(3 * V), part(F)
        xb, y = part(F), part(F)
        o1, o1s, s0 = acc[:, 0:12 * V], acc[:, 12 * V:15 * V], acc[:, 15 * V:17 * V]
        st6, mv, jk = (acc[:, 17 * V + o:17 * V + o + k] for o, k in ((0, 6), (8, 4), (12, 1)))
        hT = rw1.rearrange("p s r -> p (s r)").bitcast(f32)[:, 0:2 * P]
        tS = base[:, 0:TW]
        fh, fT, fo, fx = (room[:, k * 512:k * 512 + n] for k, n in ((0, F), (1, 2 * P), (2, F), (3, F)))

        def loop(eng, n0, n1):
            return eng.Fori(n0, n1)

        def pairs(eng, node):
            node(0, 0, first=True)
            node(1, 1)
            with loop(eng, 1, (NB - 1) // 2) as i:
                node(i * 2, 0)
                node(i * 2 + 1, 1)
            for b in range((NB - 1) // 2 * 2, NB):
                node(b, b % 2)

        block = ctx.enter_context(nc.Block())

        def send(sp, l):
            r, rec = ((R0, rec0), (R1, rec1))[l]
            sp.wait_ge(pos_stored, 16 * (l + 1))

            def one(j, h, first):
                k = j * 2 + h
                if not first:
                    sp.wait_ge(pos_stored, 16 * (l + 1))
                    sp.wait_ge(sent[l][h], j * (16 * CH))
                sp.dma_start(spos[:, h, :], posD[l][:, ds(k * CH, CH)]).then_inc(piece[l][h], 16)
                sp.dma_start(srec[:, h, 0:CH * r], rec[:, ds(k * (CH * r), CH * r)]).then_inc(piece[l][h], 16)

            for h in range(2):
                one(0, h, True)
            with loop(sp, 1, PIECES // 2) as j:
                for h in range(2):
                    one(j, h, False)

        def load_tables(sp, l):
            sp.wait_ge(tabs_stored, 48 * (l + 1))
            if l == 1:
                sp.wait_ge(added[0], W)
            sp.dma_start(tab[0:1, 0:W], tabD[l][0:1, 0:W]).then_inc(tab_in, 16)
            sp.dma_start(tab[0:1, W:2 * W], tabD[l][1:2, 0:W]).then_inc(tab_in, 16)
            sp.dma_start(base[:, :], baseD[l][0:1, 0:W].to_broadcast((P, W))).then_inc(tab_in, 16)
            sp.wait_ge(tab_in, 48 * (l + 1))
            sp.wait_ge(tail_stored, 32)
            for h in range(2):
                sp.wait_ge(sent[l][h], 16 * CH * (PIECES // 2))

        def windows(sp, l):
            r = (R0, R1)[l]

            def one(it, s, first):
                w = it * SLOTS + s
                start = sp.value_load(tab[0:1, ds(w, 1)], min_val=0, max_val=EN)
                if not first:
                    sp.wait_ge((summed[0], msg)[l], w - SLOTS + 1)
                dst = rw0[:, s, :, :].rearrange("p c r -> p (c r)") if l == 0 else rw1[:, s, :]
                sp.dma_start(dst, eD[l][ds(start, SW), :].rearrange("(p c) r -> p (c r)", c=2)).then_inc(rec_in[l][s], 16)

            for s in range(SLOTS):
                one(0, s, True)
            with loop(sp, 1, W // SLOTS) as it:
                for s in range(SLOTS):
                    one(it, s, False)

        def nodes_io(sp):
            def rows(b):
                sp.wait_ge(t_sb, b + 1)
                sp.dma_start(tD[ds(b * P, P), :], tS).then_inc(u_t_out, 16)

            def one(b, first):
                if not first:
                    sp.wait_ge(y_done, b)
                sp.dma_start(xb, xin[ds(b * P, P), :]).then_inc(u_x_in, 16)
                if not first:
                    rows(b - 1)
                sp.wait_ge(y_done, b + 1)
                sp.dma_start(x2D[ds(b * P, P), :], y).then_inc(u_x2_out, 16)

            one(0, True)
            with loop(sp, 1, NB) as b:
                one(b, False)
            rows(NB - 1)

        @block.sync
        def _(sp):
            sp.dma_start(keys.bitcast(i32), key0).then_inc(in_key[0], 16)
            sp.dma_start(cst[:, :], const).then_inc(in_c, 16)
            sp.dma_start(xs, xin.rearrange("(b p) f -> p b f", p=P)).then_inc(in_x, 16)
            sp.dma_start(ws[:, :], wsmall).then_inc(in_ws, 16)
            sp.dma_start(scl, wscale).then_inc(in_ws, 16)
            sp.wait_ge(tail_ready, 3)
            for l, r in ((0, R0), (1, R1)):
                sp.dma_start(eD[l][EN:EN + SW, :].rearrange("(p c) r -> p (c r)", c=2),
                             tail[:, 0:2 * r]).then_inc(tail_stored, 16)
            for l in range(2):
                sp.wait_ge(pos_ready, l + 1)
                sp.dma_start(posD[l], posi.bitcast(i32)).then_inc(pos_stored, 16)
                sp.wait_ge(tabs_ready, l + 1)
                sp.dma_start(tabD[l][0, :].rearrange("(q p) -> p q", p=P), wsti).then_inc(tabs_stored, 16)
                sp.dma_start(tabD[l][1, :].rearrange("(q p) -> p q", p=P), wbi).then_inc(tabs_stored, 16)
                sp.dma_start(baseD[l][0, :].rearrange("(q p) -> p q", p=P), wbase).then_inc(tabs_stored, 16)
                if l == 0:
                    sp.dma_start(keys.bitcast(i32), key1).then_inc(in_key[1], 16)
                    sp.wait_ge(h_ready, 1)
                    sp.dma_start(hD.rearrange("(b p) f -> p b f", p=P), hS[:, :, :]).then_inc(h_stored, 16)
                    send(sp, 0)
            load_tables(sp, 0)
            windows(sp, 0)
            sp.wait_ge(summed[0], W)
            sp.dma_start(room[:, 0:S * S // 2 + V * V], wbig).then_inc(wbig_in, 16)
            nodes_io(sp)
            sp.wait_ge(u_t_out, 16 * NB)
            load_tables(sp, 1)
            windows(sp, 1)
            sp.wait_ge(u_x2_out, 16 * NB)

            def block_in(b, first):
                if not first:
                    sp.wait_ge(f_dve, b * 4)
                sp.dma_start(fx, x2D[ds(b * P, P), :]).then_inc(f_x_in, 16)
                sp.wait_ge(f_dve, (b + 1) * 4)
                sp.dma_start(out[ds(b * P, P), :], fo).then_inc(f_out, 16)

            sp.wait_ge(added[1], W)
            block_in(0, True)
            with loop(sp, 1, NB) as b:
                block_in(b, False)
            sp.wait_ge(f_out, 16 * NB)

        @block.gpsimd
        def _(pool):
            def scatter(l, load):
                r = (R0, R1)[l]

                def one(j, h):
                    pool.wait_ge(piece[l][h], (j + 1) * 32)
                    pool.sem_inc(pool_go, 1)
                    for k in range(CH):
                        nc.gpsimd.indirect_dma_start(
                            out=eD[l], out_offset=bass.IndirectOffsetOnAxis(ap=spos[:, h, k:k + 1], axis=0),
                            in_=srec[:, h, k * r:(k + 1) * r], in_offset=None).then_inc(sent[l][h], 16)

                if load:
                    def fetch(j, h, first):
                        k = j * 2 + h
                        if not first:
                            pool.wait_ge(sent[l][h], j * (16 * CH))
                        pool.dma_start(spos[:, h, :], posD[l][:, ds(k * CH, CH)]).then_inc(piece[l][h], 16)
                        pool.dma_start(srec[:, h, 0:CH * r], rec1[:, ds(k * (CH * r), CH * r)]).then_inc(piece[l][h], 16)

                    pool.wait_ge(pos_stored, 32)
                    for h in range(2):
                        pool.wait_ge(sent[0][h], 16 * CH * (PIECES // 2))
                    fetch(0, 0, True)
                    fetch(0, 1, True)
                    one(0, 0)
                    with loop(pool, 1, PIECES // 2) as j:
                        fetch(j, 0, False)
                        one(j - 1, 1)
                        fetch(j, 1, False)
                        one(j, 0)
                    one(PIECES // 2 - 1, 1)
                    for h in range(2):
                        pool.wait_ge(sent[l][h], 16 * CH * (PIECES // 2))
                else:
                    with loop(pool, 0, PIECES // 2) as j:
                        for h in range(2):
                            one(j, h)

            def gather(l):
                table = (hD, tD)[l]

                def one(it, s, first):
                    w = it * SLOTS + s
                    pool.wait_ge(rec_in[l][s], (it + 1) * 16)
                    if not first:
                        pool.wait_ge((summed[0], msg)[l], w - SLOTS + 1)
                    pool.sem_inc(pool_go, 1)
                    for c in range(2):
                        if l == 0:
                            dst, idx = xu[:, s, c, 0:F], rw0[:, s, c, 0:1]
                        else:
                            dst, idx = tb[:, s, c, :], rw1[:, s, c * R1:c * R1 + 1]
                        nc.gpsimd.indirect_dma_start(
                            out=dst, out_offset=None, in_=table,
                            in_offset=bass.IndirectOffsetOnAxis(ap=idx, axis=0)).then_inc(row_in[l][s], 16)

                for s in range(SLOTS):
                    one(0, s, True)
                with loop(pool, 1, W // SLOTS) as it:
                    for s in range(SLOTS):
                        one(it, s, False)

            scatter(0, False)
            pool.wait_ge(h_stored, 16)
            gather(0)
            scatter(1, True)
            pool.wait_ge(u_t_out, 16 * NB)
            pool.wait_ge(u_x2_out, 16 * NB)
            gather(1)

        @block.vector
        def _(dve):
            v = nc.vector

            class Steps:
                def __init__(self, s, start=0):
                    self.s, self.n, self.start = s, 0, start

                def inc(self, ins):
                    self.n += 1
                    ins.then_inc(self.s, 1)

                def link(self, ins):
                    self.inc(ins)
                    dve.wait_ge(self.s, self.start + self.n)

            c = Steps(dv)
            c.inc(v.memset(tail, 0))
            dve.wait_ge(dv, 1)
            for k in (1, R0 + 1, R1 + 1):
                v.memset(tail[:, k:k + 1], 2 * NN).then_inc(tail_ready, 1)

            def ranks(l):
                dve.wait_ge(in_key[l], 16)
                if l:
                    dve.wait_ge(pos_stored, 16)
                    dve.wait_ge(tabs_stored, 48)
                c.link(v.tensor_scalar(blki.bitcast(i32), keys.bitcast(i32), 7, None, ALU.arith_shift_right))
                c.link(v.tensor_copy(blkf, blki.bitcast(i32)))
                v.memset(junk[:, 2:3], 0.0).then_inc(dv_cnt[l], 1)
                with loop(dve, 0, NBE) as b:
                    dve.wait_ge(dv_cnt[l], b + 1)
                    v.tensor_scalar(eq[0], blkf, iota[:, ds(b, 1)], 0.0, ALU.is_equal, ALU.add,
                                    accum_out=cnt[:, ds(b, 1)]).then_inc(dv_cnt[l], 1)
                dve.wait_ge(dv_cnt[l], NBE + 1)
                c.inc(v.memset(junk[:, 0:1], 0.0))
                dve.wait_ge(dv, c.n)
                v.memset(junk[:, 0:1], 0.0).then_inc(cnt_ready, 1)
                dve.wait_ge(off_ready, l + 1)
                c.link(v.tensor_copy(tot, ps[:, 0, 64:64 + NBE]))
                c.link(v.tensor_tensor_scan(incl, ones[:, 0:NBE], tot, 0.0, ALU.mult, ALU.add))
                c.link(v.tensor_tensor(exc, incl, tot, ALU.subtract))
                c.link(v.tensor_tensor(off, exc, ps[:, 0, 0:NBE], ALU.add))
                c.link(v.tensor_scalar(off, off, -1.0, None, ALU.add))
                v.tensor_scalar(eq[0], blkf, iota[:, 0:1], None, ALU.is_equal).then_inc(dv_rank[l], 1)
                with loop(dve, 0, NBE // 2) as j:
                    for h in range(2):
                        b = j * 2 + h
                        n = j * 6 + h * 3 + 1
                        dve.wait_ge(dv_rank[l], n)
                        v.tensor_tensor_scan(run[h], ones[:, 0:1].to_broadcast((P, EC)), eq[h], off[:, ds(b, 1)],
                                             ALU.mult, ALU.add).then_inc(dv_rank[l], 1)
                        dve.wait_ge(dv_rank[l], n + 1)
                        v.tensor_scalar(eq[1 - h], blkf, iota[:, ds(b + 1, 1)], None, ALU.is_equal).then_inc(dv_rank[l], 1)
                        v.copy_predicated(rank, eq[h].bitcast(i32), run[h]).then_inc(dv_rank[l], 1)
                dve.wait_ge(dv_rank[l], 3 * NBE + 1)
                v.tensor_copy(posi.bitcast(i32), rank).then_inc(pos_ready, 1)
                c.link(v.tensor_scalar(nwin, tot, float(SW - 1), None, ALU.add))
                c.link(v.tensor_copy(nwi.bitcast(i32), nwin))
                c.link(v.tensor_scalar(nwi.bitcast(i32), nwi.bitcast(i32), SW.bit_length() - 1, None, ALU.arith_shift_right))
                c.link(v.tensor_copy(nwin, nwi.bitcast(i32)))
                c.link(v.tensor_tensor_scan(wend, ones[:, 0:NBE], nwin, 0.0, ALU.mult, ALU.add))
                c.link(v.scalar_tensor_tensor(pad, nwin, float(SW), tot, ALU.mult, ALU.subtract))
                for q in range(Q):
                    i = cst[:, C_WIN + q:C_WIN + q + 1]
                    c.link(v.tensor_scalar(mask[:, 0:NB], wend[:, 0:NB], i, None, ALU.is_le))
                    c.link(v.tensor_reduce(wb_[:, q:q + 1], mask[:, 0:NB], AX.X, ALU.add))
                    c.link(v.tensor_tensor(mask[:, 0:NB], mask[:, 0:NB], pad[:, 0:NB], ALU.mult))
                    c.link(v.tensor_reduce(wpad[:, q:q + 1], mask[:, 0:NB], AX.X, ALU.add))
                c.link(v.scalar_tensor_tensor(wst, cst[:, C_WIN:C_WIN + Q], float(SW), wpad, ALU.mult, ALU.subtract))
                c.link(v.tensor_scalar(wst, wst, float(EN), None, ALU.min))
                c.link(v.tensor_scalar(wb_, wb_, float(NB - 1), None, ALU.min))
                c.link(v.tensor_scalar(wbase, wb_, float(P), None, ALU.mult))
                c.link(v.tensor_copy(wsti, wst))
                c.link(v.tensor_copy(wbi, wb_))
                v.memset(junk[:, 1:2], 0.0).then_inc(tabs_ready, 1)

            dve.wait_ge(in_c, 16)
            ranks(0)
            dve.wait_ge(in_ws, 32)
            c.link(v.tensor_tensor(ws[:, :], ws[:, :], scl, ALU.mult))
            dve.wait_ge(in_x, 16)
            with loop(dve, 0, NB) as b:
                v.bn_stats(stats[:, ds(b, 1), :].rearrange("p b s -> p (b s)"),
                           xs[:, ds(b, 1), :].rearrange("p b s -> p (b s)")).then_inc(dv_bn, 1)
            dve.wait_ge(dv_bn, NB)
            me, mo, ve, vo = (stats[:, :, k:k + 1].rearrange("p b s -> p (b s)") for k in (1, 4, 2, 5))
            c.link(v.tensor_tensor(mean, me, mo, ALU.add))
            c.link(v.tensor_scalar(mean, mean, 0.5, None, ALU.mult))
            c.link(v.tensor_tensor(tmpn, me, mean, ALU.subtract))
            c.link(v.tensor_tensor(tmpn, tmpn, tmpn, ALU.mult))
            c.link(v.tensor_tensor(var, ve, vo, ALU.add))
            c.link(v.tensor_scalar(var, var, 1.0 / F, EPS, ALU.mult, ALU.add))
            v.tensor_tensor(var, var, tmpn, ALU.add).then_inc(var_ready, 1)
            dve.wait_ge(std_ready, 1)
            c.link(v.reciprocal(rstd, tmpn))

            def over(a):
                return a.rearrange("p (b o) -> p b o", o=1).to_broadcast((P, NB, F))

            c.link(v.tensor_tensor(hS[:, :, :], xs, over(mean), ALU.subtract))
            c.link(v.tensor_tensor(hS[:, :, :], hS[:, :, :], over(rstd), ALU.mult))
            v.tensor_scalar(hS[:, :, :], hS[:, :, :], 0.0, None, ALU.max).then_inc(h_ready, 1)
            ranks(1)
            dve.wait_ge(pos_stored, 32)
            dve.wait_ge(tabs_stored, 96)
            dve.wait_ge(tail_stored, 32)
            dve.wait_ge(h_ready, 1)
            c.link(v.memset(acc[:, :], 0.0))
            dve.wait_ge(tab_in, 48)

            def products(it, s):
                dve.wait_ge(row_in[0][s], (it + 1) * 32)
                w = it * SLOTS + s
                dve.wait_ge(key_done[0], w + 1)
                for cc in range(2):
                    v.tensor_scalar(oh[:, s, cc, :], iota, base[:, ds(w, 1)], keyf[:, s, cc:cc + 1],
                                    ALU.add, ALU.is_equal).then_inc(built[0], 1)
                rr = rw0[:, s, :, 2:5].bitcast(f32)
                x0r = xu[:, s, :, 2 * F:2 * F + 3 * S].rearrange("p c (k u) -> p c k u", k=3)
                v.tensor_tensor(x0r, xu[:, s, :, 0:S].rearrange("p c (o u) -> p c o u", o=1).to_broadcast((P, 2, 3, S)),
                                rr.rearrange("p c (k o) -> p c k o", o=1).to_broadcast((P, 2, 3, S)), ALU.mult).then_inc(built[0], 1)
                x1r = xu[:, s, :, 2 * F + 3 * S:A0].rearrange("p c (u k) -> p c u k", k=3)
                v.tensor_tensor(x1r, xu[:, s, :, S:F].rearrange("p c (u k) -> p c u k", k=3),
                                rr.rearrange("p c (o k) -> p c o k", o=1).to_broadcast((P, 2, V, 3)), ALU.mult).then_inc(built[0], 1)

            def add(l, w, s, first):
                blk = dve.value_load(tab[0:1, ds(w + W, 1)], min_val=0, max_val=NB - 1)
                dve.wait_ge(summed[l], w + 1)
                if not first:
                    dve.wait_ge(added[l], w)
                if l == 0:
                    a = acc[:, ds(blk * A0, A0)].rearrange("p (j f) -> p j f", j=2)
                    t = ps[:, 2 * (s % 2):2 * (s % 2) + 2, 0:HALF]
                else:
                    a, t = acc1[:, ds(blk * F, F)], ps[:, s % 2, 0:F]
                v.tensor_tensor(a, a, t, ALU.add).then_inc(added[l], 1)

            for s in range(SLOTS):
                products(0, s)
                if s:
                    add(0, s - 1, s - 1, s == 1)
            with loop(dve, 1, W // SLOTS) as it:
                for s in range(SLOTS):
                    products(it, s)
                    add(0, it * SLOTS + s - 1, (s - 1) % SLOTS, False)
            add(0, W - 1, SLOTS - 1, False)
            dve.wait_ge(added[0], W)

            U_DVE = 17

            def normalised(b, k):
                if k == 0:
                    dve.wait_ge(u_std, b + 1)
                    v.reciprocal(mv[:, 3:4], mv[:, 2:3]).then_inc(u_norm, 1)
                elif k == 1:
                    dve.wait_ge(u_norm, b * 2 + 1)
                    v.tensor_scalar(hb, y, mv[:, 0:1], mv[:, 3:4], ALU.subtract, ALU.mult).then_inc(u_norm, 1)
                else:
                    dve.wait_ge(u_norm, b * 2 + 2)
                    v.tensor_scalar(hb, hb, 0.0, None, ALU.max).then_inc(h2_done, 1)

            def node(b, p, first=False):
                n = Steps(u_dve, b * U_DVE)

                def after(step):
                    dve.wait_ge(u_dve, n.start + step)

                h = hS[:, ds(b, 1), :].rearrange("p b f -> p (b f)")
                x1 = hS[:, ds(b, 1), S:F].rearrange("p b (u k) -> p (b u) k", k=3)
                a1 = aS[p][:, S:F].rearrange("p (u k) -> p u k", k=3)

                def z0_product(j):
                    dve.wait_ge(z0_mm, b * 8 + j + 1)
                    if not (first and j < 2):
                        dve.wait_ge(z0_sum, b * 8 + j - 1)
                    u = 32 * (j % 2) + 8 * (j // 2)
                    v.tensor_tensor(pz[:, 512 * (j % 2):512 * (j % 2) + 512].rearrange("p (u w) -> p u w", w=S),
                                    ps[:, 2 + j % 2, :].rearrange("p (u w) -> p u w", w=S),
                                    hS[:, ds(b, 1), u:u + 8].rearrange("p b (u o) -> p (b u) o", o=1).to_broadcast((P, 8, S)),
                                    ALU.mult).then_inc(z0_prod, 1)

                gv, tv = (t.rearrange("p (u w) -> p u w", u=V) for t in (g, mb[:, 0:1024]))

                def g_product(dst, k):
                    n.inc(v.tensor_tensor(dst, x1[:, :, k:k + 1].to_broadcast((P, V, V)),
                                          a1[:, :, k:k + 1].rearrange("p u o -> p o u").to_broadcast((P, V, V)), ALU.mult))

                dve.wait_ge(agg_sb, b + 1)
                if not first:
                    dve.wait_ge(out_mm, b)
                g_product(gv, 0)
                g_product(tv, 1)
                z0_product(0)
                after(2)
                n.inc(v.tensor_tensor(g, g, mb[:, 0:1024], ALU.add))
                if not first:
                    normalised(b - 1, 0)
                after(3)
                g_product(tv, 2)
                if not first:
                    normalised(b - 1, 1)
                z0_product(1)
                if not first:
                    normalised(b - 1, 2)
                after(4)
                v.tensor_tensor(g, g, mb[:, 0:1024], ALU.add).then_inc(g_done, 1)

                def out1(u):
                    dve.wait_ge(z1_mm, b * 4 + u + 1)
                    if u == 0:
                        dve.wait_ge(g_done, b + 1)
                    else:
                        after(4 + u)
                    lo = 16 * (u // 2)
                    cf = (a1, x1)[u % 2][:, lo:lo + 16, :].rearrange("p (u o) k -> p k u o", o=1)
                    v.tensor_tensor(mb.rearrange("p (k j w) -> p k j w", k=3, w=V),
                                    ps[:, u % 2, :].rearrange("p (o j w) -> p o j w", o=1, w=V).to_broadcast((P, 3, 16, V)),
                                    cf.to_broadcast((P, 3, 16, V)), ALU.mult).then_inc(z1_used, 1)

                def out1_sum(u):
                    dve.wait_ge(z1_used, b * 4 + u + 1)
                    n.inc(v.tensor_reduce(o1[:, u * 3 * V:(u + 1) * 3 * V].rearrange("p (k w) -> p k w", k=3),
                                          mb.rearrange("p (k j w) -> p k w j", k=3, w=V), AX.X, ALU.add))

                out1(0)
                z0_product(2)
                out1_sum(0)
                z0_product(3)
                out1(1)
                z0_product(4)
                out1_sum(1)
                out1(2)
                z0_product(5)
                out1_sum(2)
                z0_product(6)
                out1(3)
                z0_product(7)
                out1_sum(3)
                dve.wait_ge(z0_sum, b * 8 + 8)
                n.inc(v.tensor_reduce(s0, ps[:, 4, :].rearrange("p (u w) -> p w u", w=S), AX.X, ALU.add))
                after(8)
                n.inc(v.tensor_reduce(o1s, o1.rearrange("p (u c) -> p c u", u=4), AX.X, ALU.add))
                po = ps[:, 7, 0:F]
                dve.wait_ge(out_mm, b + 1)
                if not first:
                    dve.wait_ge(u_x2_out, b * 16)
                    dve.wait_ge(h2_done, b)
                after(9)
                n.inc(v.scalar_tensor_tensor(y[:, 0:S], s0, 5120.0 ** -0.5, po[:, 0:S], ALU.mult, ALU.add))
                after(10)
                n.inc(v.scalar_tensor_tensor(y[:, S:F].rearrange("p (w k) -> p k w", k=3),
                                             o1s.rearrange("p (k w) -> p k w", k=3), 1.0 / 64,
                                             po[:, S:F].rearrange("p (w k) -> p k w", k=3), ALU.mult, ALU.add))
                dve.wait_ge(u_x_in, (b + 1) * 16)
                n.inc(v.tensor_tensor(xb, xb, h, ALU.add))
                after(13)
                v.tensor_tensor(y, y, xb, ALU.add).then_inc(y_done, 1)
                dve.wait_ge(y_done, b + 1)
                n.inc(v.memset(jk, 0.0))
                n.inc(v.bn_stats(st6, y))
                after(15)
                n.inc(v.memset(jk, 0.0))
                n.inc(v.bn_aggr(mv[:, 0:2], st6))
                after(17)
                v.tensor_scalar(mv[:, 2:3], mv[:, 1:2], EPS, None, ALU.add).then_inc(u_var, 1)
                assert n.n == U_DVE, n.n

            pairs(dve, node)
            for k in range(3):
                normalised(NB - 1, k)

            dve.wait_ge(tab_in, 96)
            dve.wait_ge(h2_kept, NB)
            c.link(v.memset(acc1, 0.0))

            def messages(it, s, first):
                w = it * SLOTS + s
                t2 = s % 2
                dve.wait_ge(key_done[1], w + 1)
                if not first:
                    dve.wait_ge(summed[1], w - 1)
                for cc in range(2):
                    v.tensor_scalar(oh1[:, t2, cc, :], iota, base[:, ds(w, 1)], keyf[:, s, cc:cc + 1],
                                    ALU.add, ALU.is_equal).then_inc(built[1], 1)
                dve.wait_ge(row_in[1][s], (it + 1) * 32)
                dve.wait_ge(scaled[1], (w + 1) * 2)
                n0 = w * 10
                ev = [[rw1[:, s, cc * R1 + 3 + d:cc * R1 + 4 + d].bitcast(f32) for d in range(3)] for cc in range(2)]
                for k, (d, o, n, t) in enumerate(((0, 0, S + V, F + S), (1, V, S + V, F), (2, V, S, F + 160), (2, S + 2 * V, V, F + S))):
                    for cc in range(2):
                        if k in (1, 2):
                            dve.wait_ge(built[1], n0 + 2 + 2 * (k - 1) + cc + 1)
                        m = mg[:, t2, cc, o:o + n]
                        v.scalar_tensor_tensor(m, tb[:, s, cc, t:t + n], ev[cc][d], m, ALU.mult, ALU.add).then_inc(built[1], 1)
                dve.wait_ge(gate_done, w + 1)
                dve.wait_ge(built[1], n0 + 10)
                m = mg[:, t2, :, :].rearrange("p c f -> p (c f)")
                v.tensor_tensor(m, m, gt[:, t2, :], ALU.mult).then_inc(msg, 1)

            for s in range(SLOTS):
                messages(0, s, s < 2)
                if s:
                    add(1, s - 1, s - 1, s == 1)
            with loop(dve, 1, W // SLOTS) as it:
                for s in range(SLOTS):
                    messages(it, s, False)
                    add(1, it * SLOTS + s - 1, (s - 1) % SLOTS, False)
            add(1, W - 1, SLOTS - 1, False)
            dve.wait_ge(added[1], W)

            def last(b, first):
                n = Steps(f_dve, b * 4)
                if not first:
                    dve.wait_ge(f_pe, (b - 1) * 2 + 1)
                a = acc1[:, ds(b * F, F)]
                h = hS[:, ds(b, 1), :].rearrange("p b f -> p (b f)")
                hv = hS[:, ds(b, 1), S:F].rearrange("p b (u k) -> p (b k) u", k=3)
                n.inc(v.tensor_tensor(fh[:, V:V + S], a[:, V:V + S], h[:, 0:S], ALU.add))
                n.inc(v.tensor_tensor(fh[:, 0:V], a[:, 0:V], hv[:, 0, :], ALU.add))
                n.inc(v.tensor_tensor(fh[:, S + V:F].rearrange("p (k u) -> p k u", u=V),
                                      a[:, S + V:F].rearrange("p (k u) -> p k u", u=V), hv[:, 1:3, :], ALU.add))
                dve.wait_ge(f_x_in, (b + 1) * 16)
                dve.wait_ge(f_pe, b * 2 + 2)
                if not first:
                    dve.wait_ge(f_out, b * 16)
                n.inc(v.tensor_tensor(fo, ps[:, 7, 0:F], fx, ALU.add))

            last(0, True)
            with loop(dve, 1, NB) as b:
                last(b, False)

        @block.scalar
        def _(act):
            a = nc.scalar
            act.wait_ge(var_ready, 1)
            a.activation(tmpn, var, ACT.Sqrt).then_inc(std_ready, 1)

            def dist(it, s, first):
                w = it * SLOTS + s
                act.wait_ge(rec_in[0][s], (it + 1) * 16)
                if not first:
                    act.wait_ge(built[0], (w - SLOTS + 1) * 4)
                a.activation(keyf[:, s, :], rw0[:, s, :, 1:2].rearrange("p c o -> p (c o)"), ACT.Copy).then_inc(key_done[0], 1)
                act.wait_ge(row_in[0][s], (it + 1) * 32)
                for cc in range(2):
                    a.activation(xu[:, s, cc, F:2 * F], xu[:, s, cc, 0:F], ACT.Copy,
                                 scale=rw0[:, s, cc, 5:6].bitcast(f32)).then_inc(scaled[0], 1)

            for s in range(SLOTS):
                dist(0, s, True)
            with loop(act, 1, W // SLOTS) as it:
                for s in range(SLOTS):
                    dist(it, s, False)

            def ahead(b, p, first=False):
                h = hS[:, ds(b, 1), :].rearrange("p b f -> p (b f)")
                if not first:
                    act.wait_ge(agg_mm, b)
                    act.wait_ge(h_t, b)
                a.activation(ab, acc[:, ds(b * A0, A0)], ACT.Copy).then_inc(agg_c, 1)
                a.activation(x1b, h[:, S:F], ACT.Copy)
                a.activation(cat[:, S:2 * S], h[:, 0:S], ACT.Copy)
                act.wait_ge(agg_t, b + 1)
                a.activation(aT[:, 0:4 * P], ps[:, 5, :], ACT.Copy)
                a.activation(aT[0:A0 - 4 * P, 4 * P:5 * P], ps[0:A0 - 4 * P, 6, 0:P], ACT.Copy).then_inc(agg_t_sb, 1)
                act.wait_ge(agg_mm, b + 1)
                a.activation(cat[:, 0:S], ps[:, 5, 0:S], ACT.Copy)
                a.activation(cat[:, 2 * S:3 * S], ps[:, 5, 0:S], ACT.Copy)
                if not first:
                    act.wait_ge(y_done, b - 1)
                    act.wait_ge(out_mm, b - 1)
                a.activation(aS[p], ps[:, 5, 0:F], ACT.Copy).then_inc(agg_sb, 1)
                act.wait_ge(h_t, b + 1)
                a.activation(catT[p], ps[:, 6, 0:P], ACT.Copy)
                a.activation(catU[p], ps[:, 6, P:2 * P], ACT.Copy)
                a.activation(x1T[p][0:3 * V, :], ps[0:3 * V, 6, 2 * P:3 * P], ACT.Copy).then_inc(h_t_sb, 1)

            def std(b):
                act.wait_ge(u_var, b + 1)
                a.activation(mv[:, 2:3], mv[:, 2:3], ACT.Sqrt).then_inc(u_std, 1)

            def behind(b, first=False):
                act.wait_ge(h2_t, b + 1)
                a.activation(hT[:, 0:P], ps[:, 5, 0:P], ACT.Copy)
                a.activation(hT[0:V, P:2 * P], ps[0:V, 5, P:2 * P], ACT.Copy).then_inc(h2_t_sb, 1)
                a.activation(hS[:, ds(b, 1), :].rearrange("p b f -> p (b f)"), hb, ACT.Copy).then_inc(h2_kept, 1)
                act.wait_ge(t_mm, b + 1)
                if not first:
                    act.wait_ge(u_t_out, b * 16)
                a.activation(tS, ps[:, 6, 0:TW], ACT.Copy).then_inc(t_sb, 1)

            def node(b, p, first=False):
                last = isinstance(b, int) and b == NB - 1
                if not first:
                    std(b - 1)
                if not last:
                    ahead(b + 1, 1 - p, first)
                act.wait_ge(g_t, b + 1)
                a.activation(g, ps[:, 5:7, :].rearrange("p a f -> p (a f)"), ACT.Copy).then_inc(g_t_sb, 1)
                if not first:
                    behind(b - 1, isinstance(b, int) and b == 1)

            act.wait_ge(added[0], W)
            ahead(0, 0, True)
            pairs(act, node)
            std(NB - 1)
            behind(NB - 1)

            def gates(it, s, first):
                w = it * SLOTS + s
                t2 = s % 2
                act.wait_ge(rec_in[1][s], (it + 1) * 16)
                if not (first and s < SLOTS):
                    act.wait_ge(msg, w - SLOTS + 1)
                a.activation(keyf[:, s, :], rw1[:, s, :].rearrange("p (c r) -> p c r", c=2)[:, :, 1:2].rearrange("p c o -> p (c o)"),
                             ACT.Copy).then_inc(key_done[1], 1)
                act.wait_ge(attr_t, w + 1)
                if not (first and s < 2):
                    act.wait_ge(gate_mm, w - 1)
                a.activation(atr[0:2 * R1, t2, :], ps[0:2 * R1, 4 + t2, 0:P], ACT.Copy).then_inc(attr_c, 1)
                if not (first and s < 2):
                    act.wait_ge(msg, w - 1)
                act.wait_ge(gate_mm, w + 1)
                a.activation(gt[:, t2, :].rearrange("p (c f) -> p c f", c=2), ps[:, 2 + 4 * t2:4 + 4 * t2, 0:F], ACT.Sigmoid).then_inc(gate_done, 1)
                if not (first and s < 2):
                    act.wait_ge(summed[1], w - 1)
                act.wait_ge(row_in[1][s], (it + 1) * 32)
                for cc in range(2):
                    a.activation(mg[:, t2, cc, :], tb[:, s, cc, 0:F], ACT.Copy,
                                 scale=rw1[:, s, cc * R1 + 2:cc * R1 + 3].bitcast(f32)).then_inc(scaled[1], 1)

            for s in range(SLOTS):
                gates(0, s, True)
            with loop(act, 1, W // SLOTS) as it:
                for s in range(SLOTS):
                    gates(it, s, False)

            with loop(act, 0, NB) as b:
                act.wait_ge(f_pe, b * 2 + 1)
                a.activation(fT[:, 0:P], ps[:, 5, 0:P], ACT.Copy)
                a.activation(fT[0:V, P:2 * P], ps[0:V, 5, P:2 * P], ACT.Copy).then_inc(f_act, 1)

        @block.tensor
        def _(pe):
            t = nc.tensor

            def flip(dst, src):
                return t.matmul(dst, src, ident, start=True, stop=True)

            pe.wait_ge(in_c, 16)
            for l in range(2):
                pe.wait_ge(cnt_ready, l + 1)
                t.matmul(ps[:, 0, 0:NBE], tri, cnt, start=True, stop=True)
                t.matmul(ps[:, 0, 64:64 + NBE], ones, cnt, start=True, stop=True).then_inc(off_ready, 1)

            def sums(it, s, first):
                w = it * SLOTS + s
                pe.wait_ge(built[0], (w + 1) * 4)
                pe.wait_ge(scaled[0], (w + 1) * 2)
                if not (first and s < 2):
                    pe.wait_ge(added[0], w - 1)
                for cc in range(2):
                    for j in range(2):
                        last = t.matmul(ps[:, 2 * (s % 2) + j, 0:HALF], oh[:, s, cc, :],
                                        xu[:, s, cc, j * HALF:(j + 1) * HALF], start=(cc == 0), stop=(cc == 1))
                last.then_inc(summed[0], 1)

            for s in range(SLOTS):
                sums(0, s, True)
            with loop(pe, 1, W // SLOTS) as it:
                for s in range(SLOTS):
                    sums(it, s, False)

            pe.wait_ge(added[0], W)
            pe.wait_ge(wbig_in, 16)

            def sums_t(b):
                pe.wait_ge(agg_c, b + 1)
                for k in range(KC):
                    n = min(P, A0 - k * P)
                    last = flip(ps[0:n, 5 + k // 4, (k % 4) * P:(k % 4) * P + P], ab[:, k * P:k * P + n])
                last.then_inc(agg_t, 1)

            def aggregate(b):
                pe.wait_ge(agg_t_sb, b + 1)
                for k in range(KC):
                    n = min(P, A0 - k * P)
                    last = t.matmul(ps[:, 5, 0:F], aT[0:n, k * P:(k + 1) * P], ws[0:n, WB + k * F:WB + (k + 1) * F],
                                    start=(k == 0), stop=(k == KC - 1))
                last.then_inc(agg_mm, 1)

            def factors_t(b):
                pe.wait_ge(agg_sb, b + 1)
                flip(ps[:, 6, 0:P], cat[:, 0:P])
                flip(ps[:, 6, P:2 * P], cat[:, S:3 * S])
                flip(ps[0:3 * V, 6, 2 * P:3 * P], x1b).then_inc(h_t, 1)

            def h2_flips(b, gb=None):
                pe.wait_ge(h2_done, b + 1)
                if gb is not None:
                    pe.wait_ge(g_t_sb, gb + 1)
                flip(ps[:, 5, 0:P], hb[:, 0:P])
                flip(ps[0:V, 5, P:2 * P], hb[:, P:F]).then_inc(h2_t, 1)

            def rows(b):
                pe.wait_ge(h2_t_sb, b + 1)
                t.matmul(ps[:, 6, 0:TW], hT[:, 0:P], ws[:, WT:WT + TW], start=True, stop=False)
                t.matmul(ps[:, 6, 0:TW], hT[0:V, P:2 * P], ws[0:V, WT + TW:WT + 2 * TW], start=False, stop=True).then_inc(t_mm, 1)

            def node(b, p, first=False):
                last_block = isinstance(b, int) and b == NB - 1

                def z1(u):
                    if not (first and u < 2):
                        pe.wait_ge(z1_used, b * 4 + u - 1)
                    lo = (S, 0)[u % 2]
                    t.matmul(ps[:, u % 2, :], catT[p][lo:lo + S, :], w1x1[lo:lo + S, (u // 2) * 512:(u // 2) * 512 + 512],
                             start=True, stop=True).then_inc(z1_mm, 1)

                def z0(j):
                    if not (first and j < 2):
                        pe.wait_ge(z0_prod, b * 8 + j - 1)
                    lo = S * (j % 2)
                    t.matmul(ps[:, 2 + j % 2, :], (catT, catU)[j % 2][p][lo:lo + S, :],
                             w000[lo:lo + S, (j // 2) * 512:(j // 2) * 512 + 512], start=True, stop=True).then_inc(z0_mm, 1)

                def z0_total(j):
                    pe.wait_ge(z0_prod, b * 8 + j + 1)
                    if j == 0 and not first:
                        pe.wait_ge(y_done, b)
                    t.matmul(ps[:, 4, :], ident, pz[:, 512 * (j % 2):512 * (j % 2) + 512],
                             start=(j == 0), stop=(j == 7)).then_inc(z0_sum, 1)

                pe.wait_ge(h_t_sb, b + 1)
                z1(0)
                z1(1)
                z0(0)
                z0(1)
                if not last_block:
                    if not first:
                        if not (isinstance(b, int) and b == 1):
                            pe.wait_ge(t_sb, b - 1)
                        pe.wait_ge(g_t_sb, b)
                    sums_t(b + 1)
                z0_total(0)
                z0(2)
                if not last_block:
                    aggregate(b + 1)
                z0_total(1)
                z0(3)
                if not last_block:
                    factors_t(b + 1)
                z0_total(2)
                z0(4)
                pe.wait_ge(g_done, b + 1)
                if not last_block:
                    pe.wait_ge(h_t_sb, b + 2)
                else:
                    pe.wait_ge(t_sb, b - 1)
                for k in range(8):
                    last = flip(ps[:, 5 + k // 4, (k % 4) * P:(k % 4) * P + P], g[:, k * P:(k + 1) * P])
                last.then_inc(g_t, 1)
                z1(2)
                z0_total(3)
                z0(5)
                if not first:
                    h2_flips(b - 1, b)
                z1(3)
                z0_total(4)
                z0(6)
                if not first:
                    pe.wait_ge(y_done, b)
                t.matmul(ps[:, 7, S:F], x1T[p][0:3 * V, :], ws[0:3 * V, WU + S:WU + F], start=True, stop=True)
                t.matmul(ps[:, 7, 0:S], catU[p][0:S, :], ws[0:S, WU:WU + S], start=True, stop=False)
                pe.wait_ge(g_t_sb, b + 1)
                for k in range(8):
                    last = t.matmul(ps[:, 7, 0:S], g[:, k * P:(k + 1) * P], ws[:, W110 + k * S:W110 + (k + 1) * S],
                                    start=False, stop=(k == 7))
                last.then_inc(out_mm, 1)
                z0_total(5)
                z0(7)
                if not first:
                    rows(b - 1)
                z0_total(6)
                z0_total(7)

            sums_t(0)
            aggregate(0)
            factors_t(0)
            pairs(pe, node)
            pe.wait_ge(t_sb, NB - 1)
            h2_flips(NB - 1)
            rows(NB - 1)

            def gate(it, s, first):
                w = it * SLOTS + s
                t2 = s % 2
                pe.wait_ge(rec_in[1][s], (it + 1) * 16)
                if not (first and s < 2):
                    pe.wait_ge(attr_c, w - 1)
                flip(ps[0:2 * R1, 4 + t2, 0:P], rw1[:, s, :].bitcast(f32)).then_inc(attr_t, 1)
                pe.wait_ge(attr_c, w + 1)
                if not (first and s < 2):
                    pe.wait_ge(gate_done, w - 1)
                for cc in range(2):
                    k = slice(cc * R1, (cc + 1) * R1)
                    last = t.matmul(ps[:, 2 + 4 * t2 + cc, 0:F], atr[k, t2, :], ws[k, WG:WG + F], start=True, stop=True)
                last.then_inc(gate_mm, 1)

            def sums1(w, s, first):
                pe.wait_ge(msg, w + 1)
                if not (first and s < 2):
                    pe.wait_ge(added[1], w - 1)
                for cc in range(2):
                    last = t.matmul(ps[:, s % 2, 0:F], oh1[:, s % 2, cc, :], mg[:, s % 2, cc, :],
                                    start=(cc == 0), stop=(cc == 1))
                last.then_inc(summed[1], 1)

            pe.wait_ge(t_sb, NB)
            for s in range(SLOTS):
                gate(0, s, True)
                if s:
                    sums1(s - 1, s - 1, True)
            with loop(pe, 1, W // SLOTS) as it:
                for s in range(SLOTS):
                    gate(it, s, False)
                    sums1(it * SLOTS + s - 1, (s - 1) % SLOTS, False)
            sums1(W - 1, SLOTS - 1, False)

            def last_block(b, first):
                pe.wait_ge(f_dve, b * 4 + 3)
                if not first:
                    pe.wait_ge(f_act, b)
                flip(ps[:, 5, 0:P], fh[:, 0:P])
                flip(ps[0:V, 5, P:2 * P], fh[:, P:F]).then_inc(f_pe, 1)
                pe.wait_ge(f_act, b + 1)
                t.matmul(ps[:, 7, 0:F], fT[:, 0:P], ws[:, WF:WF + F], start=True, stop=False)
                t.matmul(ps[:, 7, 0:F], fT[0:V, P:2 * P], ws[0:V, WF + F:WF + 2 * F], start=False, stop=True).then_inc(f_pe, 1)

            pe.wait_ge(gate_done, W)
            last_block(0, True)
            with loop(pe, 1, NB) as b:
                last_block(b, False)


_ORDER = ["x", "rec0", "rec1", "key0", "key1", "wsmall", "wscale", "wbig", "const"]


def constants():
    c = np.zeros((P, CW), np.float32)
    c[:, C_ID:C_ID + P] = np.eye(P)
    c[:, C_TRI:C_TRI + P] = np.triu(np.ones((P, P)), 1)
    c[:, C_ONE:C_ONE + P] = 1.0
    c[:, C_IOTA:C_IOTA + P] = np.arange(P)
    c[:, C_WIN:C_WIN + Q] = np.arange(Q * P).reshape(Q, P).T
    return c


def place(ws, w000, w011, w101, w110, lm0, lm1, m000, m011, m101, m110, lu0, lu1, ss, sv, vs, vv, rad, bias, ls, lv):
    full = np.zeros((KC * P, F), np.float32)
    full[0:S, 0:S] = lm0
    full[F:F + S, 0:S] = m000
    for k in range(3):
        full[S + k:F:3, S + k::3] = lm1
        full[F + S + k:2 * F:3, S + k::3] = m101
        full[2 * F + k * S:2 * F + (k + 1) * S, S + k::3] = m011
        full[2 * F + 3 * S + k:A0:3, 0:S] = m110
    for k in range(KC):
        ws[:, WB + k * F:WB + (k + 1) * F] = full[k * P:(k + 1) * P]

    def two(at, m, n):
        ws[:, at:at + n] = m[0:P]
        ws[0:V, at + n:at + 2 * n] = m[P:F]

    t = np.zeros((F, TW), np.float32)
    t[0:S, V:V + S] = ss
    t[0:S, F + S:F + S + V] = sv
    for k in range(3):
        at = (0, S + V, S + 2 * V)[k]
        t[S + k::3, at:at + V] = vs
        at = (F + S + V, F, F + 160)[k]
        t[S + k::3, at:at + S] = vv
    two(WT, t, TW)
    u = np.zeros((F, F), np.float32)
    u[0:S, 0:S] = lu0
    f = np.zeros((F, F), np.float32)
    f[V:V + S, 0:S] = ls
    for k in range(3):
        u[S + k::3, S + k::3] = lu1
        at = (0, S + V, S + 2 * V)[k]
        f[at:at + V, S + k::3] = lv
    ws[0:S, WU:WU + S] = u[0:S, 0:S]
    ws[0:3 * V, WU + S:WU + F] = u[S:F, S:F]
    two(WF, f, F)
    order = [*range(S, F, 3), *range(S), *range(S + 1, F, 3), *range(S + 2, F, 3)]
    for c in range(2):
        ws[c * R1 + 6:c * R1 + 22, WG:WG + F] = rad[order].T
        ws[c * R1 + 22, WG:WG + F] = bias[order]
    for c in range(8):
        ws[:, W110 + c * S:W110 + (c + 1) * S] = w110[c * P:(c + 1) * P]


def kernel(**inputs):
    import numpy as _np
    import concourse.bacc as _bacc
    from concourse import mybir as _mybir
    from concourse.bass_utils import run_bass_kernel_spmd as _run

    g = {k: _np.asarray(a) for k, a in inputs.items()}
    one = lambda shape, value: _np.full(shape, value, _np.float32)
    x = _np.zeros((NN, F), _np.float32)
    x[0:N] = g["x"]
    src = _np.full((EN,), NN - 1, _np.int32)
    dst = _np.full((EN,), NN - 1, _np.int32)
    src[0:E], dst[0:E] = g["src"], g["dst"]
    rec1 = _np.zeros((EN, R1), _np.int32)
    rec1[:, 0], rec1[:, 1] = src, dst
    rec1[0:E, 2:6] = g["edge_attr_4"].view(_np.int32)
    rec1[0:E, 6:22] = g["edge_attr_16"].view(_np.int32)
    rec1[:, 22] = _np.ones((EN,), _np.float32).view(_np.int32)
    rec0 = _np.zeros((EN, R0), _np.int32)
    rec0[:, 0], rec0[:, 1] = dst, src
    rec0[0:E, 2:6] = g["edge_attr_4"].view(_np.int32)
    p0, p1 = "L0_gnn_", "L1_gnn_"
    wsmall, wscale = _np.zeros((P, WS), _np.float32), _np.zeros((P, WS), _np.float32)
    r2, r3 = 2.0 ** -0.5, 3.0 ** -0.5
    place(wsmall, None, None, None, g[p0 + "wu110"].reshape(V * V, S), g[p0 + "lm0"], g[p0 + "lm1"],
          g[p0 + "wm000"][:, 0], g[p0 + "wm011"][:, 0], g[p0 + "wm101"][:, 0], g[p0 + "wm110"][:, 0],
          g[p0 + "lu0"], g[p0 + "lu1"], g[p1 + "W_ss"], g[p1 + "W_sv"], g[p1 + "W_vs"], g[p1 + "W_vv"],
          g[p1 + "W_rad"], g[p1 + "b_rad"], g[p1 + "L_s"], g[p1 + "L_v"])
    m = (S + V) ** -0.5
    place(wscale, None, None, None, one((V * V, S), r3 * 5120.0 ** -0.5), S ** -0.5, V ** -0.5, m, m, m, m * r3,
          S ** -0.5, V ** -0.5, r2 * S ** -0.5, r2 * r3 * S ** -0.5, r2 * r3 * V ** -0.5, r2 * r3 * V ** -0.5,
          one((F, 16), 1.0), one((F,), 1.0), S ** -0.5, V ** -0.5)
    half = S * S // 2
    wbig = _np.zeros((P, half + V * V), _np.float32)
    w000 = g[p0 + "wu000"].transpose(1, 0, 2).reshape(S, S * S)
    wbig[0:S, 0:half], wbig[S:P, 0:half] = w000[:, 0:half], w000[:, half:]
    wbig[0:S, half:] = g[p0 + "wu101"].transpose(1, 0, 2).reshape(S, V * V)
    wbig[S:P, half:] = g[p0 + "wu011"].reshape(S, V * V)
    arrays = {"x": x, "rec0": rec0.reshape(P, EC * R0), "rec1": rec1.reshape(P, EC * R1), "key0": src.reshape(P, EC),
              "key1": dst.reshape(P, EC), "wsmall": wsmall, "wscale": wscale, "wbig": wbig, "const": constants()}
    nc = _bacc.Bacc("TRN2", target_bir_lowering=False, num_devices=1)
    args = [nc.dram_tensor(f"in_{n}", arrays[n].shape, _mybir.dt.from_np(arrays[n].dtype), kind="ExternalInput").ap()
            for n in _ORDER]
    o = nc.dram_tensor("out_0", (NN, F), _mybir.dt.float32, kind="ExternalOutput").ap()
    program(nc, *args, o)
    r = _run(nc, [{f"in_{n}": arrays[n] for n in _ORDER}], core_ids=[0])
    return r.results[0]["out_0"][0:N]
```

```python
from contextlib import ExitStack

import concourse.bass as bass
from concourse import mybir
import numpy as np

P = 128
N, E = 6250, 100000
F, S, V = 160, 64, 32
NB = -(-N // P)
NBE = NB + NB % 2
NN = NB * P
EC = -(-E // P)
EN = EC * P
SW = 2 * P
SLOTS, RSLOTS = 5, 10
W = (EN + NB * (SW - 1)) // SW
W = -(-W // RSLOTS) * RSLOTS
TURNS = W // RSLOTS
Q = -(-W // P)
R0, R1 = 8, 32
CH = 17
PIECES = EC // CH
assert PIECES * CH == EC and PIECES % 2 == 0
EARLY = 10
A0 = F + F + 3 * S + 3 * V
HALF = A0 // 2
TM = V + 3 * V
TW = TM + F
KC = -(-A0 // P)
WB = 0
WT = KC * F
WU = WT + 2 * TM
WF = WU + F
WG = WF + 2 * F
WZ = WG + F
W110 = WZ + S
WS = W110 + 8 * S
C_ID, C_TRI, C_ONE, C_IOTA, C_WIN = 0, P, 2 * P, 3 * P, 4 * P
CW = 4 * P + Q
EPS = 1e-5


def program(nc, xin, rec0, rec1, key0, key1, wsmall, wscale, wbig, const, out):
    f32, i32 = mybir.dt.float32, mybir.dt.int32
    ALU, ACT, AX = mybir.AluOpType, mybir.ActivationFunctionType, mybir.AxisListType
    ds = bass.ds
    ctx = ExitStack()
    with ctx:
        ctx.enter_context(nc.allow_non_contiguous_dma(reason="short tables"))

        def sb(name, shape, dt=f32):
            return ctx.enter_context(nc.sbuf_tensor(name, shape, dt))

        def sem(name):
            return ctx.enter_context(nc.semaphore(name))

        hD = nc.dram_tensor("h_rows", [NN, F], f32).ap()
        tD = nc.dram_tensor("t_rows", [NN, TW], f32).ap()
        x2D = nc.dram_tensor("x2_rows", [NN, F], f32).ap()
        posD = [nc.dram_tensor(f"pos{l}", [P, EC], i32).ap() for l in range(2)]
        eD = [nc.dram_tensor(f"sorted{l}", [EN + SW, r], i32).ap() for l, r in ((0, R0), (1, R1))]
        tabD = [nc.dram_tensor(f"windows{l}", [2, Q * P], i32).ap() for l in range(2)]
        baseD = [nc.dram_tensor(f"bases{l}", [1, Q * P], f32).ap() for l in range(2)]

        acc = sb("acc", [P, NB * A0])
        acc1 = acc[:, 0:NB * F]
        hS = sb("hS", [P, NB, F])
        RW = 9440
        room = sb("room", [P, RW])
        ws = sb("ws", [P, WS])
        cst = sb("cst", [P, CW])
        base = sb("base", [P, W])
        tab = sb("tab", [1, 2 * W], i32)
        rw0 = sb("rw0", [P, RSLOTS, 2, R0], i32)
        rw1 = sb("rw1", [P, RSLOTS, 2 * R1], i32)
        srec = sb("srec", [P, 2, CH * R1], i32)
        spos = sb("spos", [P, 2, CH], i32)
        keyf = sb("keyf", [P, RSLOTS, 2])
        ps = ctx.enter_context(nc.psum_tensor("ps", [P, 8, 512], f32))

        ident, tri, ones, iota = (cst[:, c:c + P] for c in (C_ID, C_TRI, C_ONE, C_IOTA))

        at = [0]

        def early(words):
            at[0] += words
            return acc[:, at[0] - words:at[0]]

        keys, blki, blkf, rank, posi = (early(EC) for _ in range(5))
        eq = [early(EC) for _ in range(2)]
        run = [early(EC) for _ in range(2)]
        scl = early(WS)
        xs = early(NB * F).rearrange("p (b f) -> p b f", f=F)
        tail = early(2 * R1).bitcast(i32)
        cnt, off, tot, incl, exc, nwin, nwi, wend, pad, mask, junk = (early(NBE) for _ in range(11))
        stats = early(NB * 6).rearrange("p (b s) -> p b s", s=6)
        mean, var, tmpn, rstd = (early(NB) for _ in range(4))
        wb_, wst, wpad, wbase = (early(Q) for _ in range(4))
        wsti, wbi = (early(Q).bitcast(i32) for _ in range(2))
        assert at[0] <= NB * A0

        in_key = [sem(f"in_key{l}") for l in range(2)]
        in_x, in_c, in_ws = sem("in_x"), sem("in_c"), sem("in_ws")
        cnt_ready, off_ready = sem("cnt_ready"), sem("off_ready")
        pos_ready, pos_stored = sem("pos_ready"), sem("pos_stored")
        tabs_ready, tabs_stored = sem("tabs_ready"), sem("tabs_stored")
        tail_ready, tail_stored = sem("tail_ready"), sem("tail_stored")
        var_ready, std_ready = sem("var_ready"), sem("std_ready")
        h_ready, h_stored = sem("h_ready"), sem("h_stored")
        acc_clear = sem("acc_clear")
        dv = sem("dv")
        dv_cnt = [sem(f"dv_cnt{l}") for l in range(2)]
        dv_rank = [sem(f"dv_rank{l}") for l in range(2)]
        dv_bn = sem("dv_bn")
        piece = [[sem(f"piece{l}{h}") for h in range(2)] for l in range(2)]
        sent = [[sem(f"sent{l}{h}") for h in range(2)] for l in range(2)]
        tab_in = sem("tab_in")
        pool_go = sem("pool_go")
        rec_in = [[sem(f"rec_in{l}{s}") for s in range(RSLOTS)] for l in range(2)]
        row_in = [[sem(f"row_in{l}{s}") for s in range(SLOTS)] for l in range(2)]
        key_done = [sem(f"key_done{l}") for l in range(2)]
        scaled = [sem(f"scaled{l}") for l in range(2)]
        built = [sem(f"built{l}") for l in range(2)]
        summed = [sem(f"summed{l}") for l in range(2)]
        added = [sem(f"added{l}") for l in range(2)]
        attr_t, attr_c, gate_mm, gate_done = sem("attr_t"), sem("attr_c"), sem("gate_mm"), sem("gate_done")
        z_in, z_sum, v_add, z_t, z_t_sb, z_mm = sem("z_in"), sem("z_sum"), sem("v_add"), sem("z_t"), sem("z_t_sb"), sem("z_mm")
        msg = sem("msg")
        wbig_in, u_x_in = sem("wbig_in"), sem("u_x_in")
        agg_c, agg_t, agg_t_sb, agg_mm, agg_sb = sem("agg_c"), sem("agg_t"), sem("agg_t_sb"), sem("agg_mm"), sem("agg_sb")
        h_t, h_t_sb, z1_mm, z1_used = sem("h_t"), sem("h_t_sb"), sem("z1_mm"), sem("z1_used")
        u_norm, u_fin, g_made = sem("u_norm"), sem("u_fin"), sem("g_made")
        w000_scaled = sem("w000_scaled")
        z0_prod, z0_t, z0_t_sb, z0_mm = sem("z0_prod"), sem("z0_t"), sem("z0_t_sb"), sem("z0_mm")
        g_done, g_t, g_t_sb = sem("g_done"), sem("g_t"), sem("g_t_sb")
        y_done, u_var, u_std, h2_done = sem("y_done"), sem("u_var"), sem("u_std"), sem("h2_done")
        h2_kept, h2_t, h2_t_sb, t_mm, t_sb = sem("h2_kept"), sem("h2_t"), sem("h2_t_sb"), sem("t_mm"), sem("t_sb")
        u_dve = sem("u_dve")
        u_t_out, u_x2_out = sem("u_t_out"), sem("u_x2_out")
        f_x_in = [sem(f"f_x_in{p}") for p in range(2)]
        f_add, f_t, f_t_sb, f_mm = sem("f_add"), sem("f_t"), sem("f_t_sb"), sem("f_mm")
        f_done, f_out = sem("f_done"), [sem(f"f_out{p}") for p in range(2)]

        xu = room[:, 0:SLOTS * 2 * A0].rearrange("p (s c f) -> p s c f", s=SLOTS, c=2)
        oh = room[:, SLOTS * 2 * A0:SLOTS * 2 * (A0 + P)].rearrange("p (s c f) -> p s c f", s=SLOTS, c=2)
        at[0] = 0

        def part(words):
            at[0] += words
            assert at[0] <= RW
            return room[:, at[0] - words:at[0]]

        tb = part(SLOTS * 2 * TW).rearrange("p (s c f) -> p s c f", s=SLOTS, c=2)
        oh1 = part(SLOTS * 2 * P).rearrange("p (s c f) -> p s c f", s=SLOTS, c=2)
        sc = part(2 * 2 * 192).rearrange("p (s c f) -> p s c f", s=2, c=2)
        mg = part(SLOTS * 2 * F).rearrange("p (s c f) -> p s c f", s=SLOTS, c=2)
        gt = part(SLOTS * 2 * F).rearrange("p (s c f) -> p s c f", s=SLOTS, c=2)
        zq, vq = (part(2 * 3 * V).rearrange("p (c v d) -> p c v d", c=2, d=3) for _ in range(2))
        atr = part(2 * P).rearrange("p (s f) -> p s f", s=2)
        zT = part(2 * 2 * P).rearrange("p (s f) -> p s f", s=2)
        at[0] = 0
        w000 = part(S * S // 2)
        w1x1 = part(V * V)
        mb = part(3 * 512)
        pz = part(3 * 512)
        gT = part(1024)
        aT = part(KC * P)
        ab = aT[:, 0:A0]
        cat = part(P)
        aS = [part(F) for _ in range(2)]
        catT = [part(P) for _ in range(2)]
        x1T = [part(P) for _ in range(2)]
        y = part(F)
        cT = [acc[:, A0:A0 + 512], part(512)]
        o1, o1s = acc[:, 0:12 * V], acc[:, 12 * V:15 * V]
        st6, mv, jk = (acc[:, 17 * V + o:17 * V + o + k] for o, k in ((0, 6), (8, 4), (12, 1)))
        rwf = rw1.rearrange("p s r -> p (s r)").bitcast(f32)
        hT, hb = rwf[:, 0:2 * P], rwf[:, 2 * P:2 * P + F]
        x1b = rwf[:, 2 * P + F:2 * P + F + 3 * V]
        xb = rw0.rearrange("p s c r -> p (s c r)").bitcast(f32)[:, 0:F]
        tS = base[:, 0:TW]
        fh, fT, fo, fx = ([room[:, (2 * k + p) * 256:(2 * k + p) * 256 + n] for p in range(2)]
                          for k, n in ((0, F), (1, 2 * P), (2, F), (3, F)))

        def loop(eng, n0, n1):
            return eng.Fori(n0, n1)

        def output_pairs(eng, ahead, behind):
            ahead(0, 0, 0)
            ahead(1, 1, 0)
            behind(0, 0, 0)
            with loop(eng, 1, (NB - 1) // 2) as i:
                ahead(i * 2, 0, i)
                behind(i * 2 - 1, 1, i - 1)
                ahead(i * 2 + 1, 1, i)
                behind(i * 2, 0, i)
            ahead(NB - 1, 0, NB // 2)
            behind(NB - 2, 1, NB // 2 - 1)
            behind(NB - 1, 0, NB // 2)

        def window_turns(eng, one):
            for s in range(RSLOTS):
                one(0, s)
            with loop(eng, 1, TURNS - 1) as it:
                for s in range(RSLOTS):
                    one(it, s)
            for s in range(RSLOTS):
                one(TURNS - 1, s)

        def at_least(eng, sem, value):
            if not isinstance(value, int) or value > 0:
                eng.wait_ge(sem, value)

        def pairs(eng, node):
            node(0, 0, first=True)
            node(1, 1)
            with loop(eng, 1, (NB - 1) // 2) as i:
                node(i * 2, 0)
                node(i * 2 + 1, 1)
            for b in range((NB - 1) // 2 * 2, NB):
                node(b, b % 2)

        block = ctx.enter_context(nc.Block())

        def store_positions(sp, l, part):
            lo, hi = ((0, EARLY * CH), (EARLY * CH, EC))[part]
            sp.wait_ge(pos_ready, 2 * l + part + 1)
            sp.dma_start(posD[l][:, lo:hi], posi[:, lo:hi].bitcast(i32)).then_inc(pos_stored, 16)

        def send(sp, part):
            def one(j, h, first):
                k = j * 2 + h
                if not first:
                    sp.wait_ge(sent[0][h], j * (16 * CH))
                sp.dma_start(spos[:, h, :], posD[0][:, ds(k * CH, CH)]).then_inc(piece[0][h], 16)
                sp.dma_start(srec[:, h, 0:CH * R0], rec0[:, ds(k * (CH * R0), CH * R0)]).then_inc(piece[0][h], 16)

            sp.wait_ge(pos_stored, 16 * (part + 1))
            if part == 0:
                for h in range(2):
                    one(0, h, True)
            with loop(sp, *((1, EARLY // 2), (EARLY // 2, PIECES // 2))[part]) as j:
                for h in range(2):
                    one(j, h, False)

        def load_tables(sp, l):
            sp.wait_ge(tabs_stored, 48 * (l + 1))
            if l == 1:
                sp.wait_ge(added[0], W)
            sp.dma_start(tab[0:1, 0:W], tabD[l][0:1, 0:W]).then_inc(tab_in, 16)
            sp.dma_start(tab[0:1, W:2 * W], tabD[l][1:2, 0:W]).then_inc(tab_in, 16)
            sp.dma_start(base[:, :], baseD[l][0:1, 0:W].to_broadcast((P, W))).then_inc(tab_in, 16)
            sp.wait_ge(tab_in, 48 * (l + 1))
            sp.wait_ge(tail_stored, 32)
            for h in range(2):
                sp.wait_ge(sent[l][h], 16 * CH * (PIECES // 2))

        def windows(sp, l):
            r = (R0, R1)[l]

            def one(it, s):
                w = it * RSLOTS + s
                start = sp.value_load(tab[0:1, ds(w, 1)], min_val=0, max_val=EN)
                at_least(sp, (summed[0], msg)[l], (1, 2)[l] * (w - RSLOTS + 1))
                dst = rw0[:, s, :, :].rearrange("p c r -> p (c r)") if l == 0 else rw1[:, s, :]
                sp.dma_start(dst, eD[l][ds(start, SW), :].rearrange("(p c) r -> p (c r)", c=2)).then_inc(rec_in[l][s], 16)

            window_turns(sp, one)

        def nodes_io(sp):
            def rows(b):
                sp.wait_ge(t_sb, b + 1)
                sp.dma_start(tD[ds(b * P, P), :], tS).then_inc(u_t_out, 16)

            def one(b, first):
                if not first:
                    sp.wait_ge(y_done, b)
                sp.dma_start(xb, xin[ds(b * P, P), :]).then_inc(u_x_in, 16)
                if not first:
                    rows(b - 1)
                sp.wait_ge(y_done, b + 1)
                sp.dma_start(x2D[ds(b * P, P), :], y).then_inc(u_x2_out, 16)

            one(0, True)
            with loop(sp, 1, NB) as b:
                one(b, False)
            rows(NB - 1)

        @block.sync
        def _(sp):
            sp.dma_start(keys.bitcast(i32), key0).then_inc(in_key[0], 16)
            sp.dma_start(cst[:, :], const).then_inc(in_c, 16)
            sp.dma_start(xs, xin.rearrange("(b p) f -> p b f", p=P)).then_inc(in_x, 16)
            sp.dma_start(ws[:, :], wsmall).then_inc(in_ws, 16)
            sp.dma_start(scl, wscale).then_inc(in_ws, 16)
            sp.wait_ge(tail_ready, 3)
            for l, r in ((0, R0), (1, R1)):
                sp.dma_start(eD[l][EN:EN + SW, :].rearrange("(p c) r -> p (c r)", c=2),
                             tail[:, 0:2 * r]).then_inc(tail_stored, 16)
            def store_tables(l):
                sp.wait_ge(tabs_ready, l + 1)
                sp.dma_start(tabD[l][0, :].rearrange("(q p) -> p q", p=P), wsti).then_inc(tabs_stored, 16)
                sp.dma_start(tabD[l][1, :].rearrange("(q p) -> p q", p=P), wbi).then_inc(tabs_stored, 16)
                sp.dma_start(baseD[l][0, :].rearrange("(q p) -> p q", p=P), wbase).then_inc(tabs_stored, 16)

            store_positions(sp, 0, 0)
            send(sp, 0)
            store_positions(sp, 0, 1)
            store_tables(0)
            send(sp, 1)
            for part in range(2):
                store_positions(sp, 1, part)
            store_tables(1)
            load_tables(sp, 0)
            windows(sp, 0)
            sp.wait_ge(summed[0], W)
            sp.dma_start(room[:, 0:S * S // 2 + V * V], wbig).then_inc(wbig_in, 16)
            nodes_io(sp)
            sp.wait_ge(u_t_out, 16 * NB)
            load_tables(sp, 1)
            windows(sp, 1)
            sp.wait_ge(u_x2_out, 16 * NB)

            def load(b, p, i):
                at_least(sp, f_done, b - 1)
                sp.dma_start(fx[p], x2D[ds(b * P, P), :]).then_inc(f_x_in[p], 16)

            def store(b, p, i):
                sp.wait_ge(f_done, b + 1)
                sp.dma_start(out[ds(b * P, P), :], fo[p]).then_inc(f_out[p], 16)

            sp.wait_ge(added[1], W)
            output_pairs(sp, load, store)
            sp.wait_ge(f_out[0], 16 * (NB - NB // 2))
            sp.wait_ge(f_out[1], 16 * (NB // 2))

        @block.gpsimd
        def _(pool):
            def scatter(l, load):
                r = (R0, R1)[l]

                def one(j, h):
                    pool.wait_ge(piece[l][h], (j + 1) * 32)
                    pool.sem_inc(pool_go, 1)
                    for k in range(CH):
                        nc.gpsimd.indirect_dma_start(
                            out=eD[l], out_offset=bass.IndirectOffsetOnAxis(ap=spos[:, h, k:k + 1], axis=0),
                            in_=srec[:, h, k * r:(k + 1) * r], in_offset=None).then_inc(sent[l][h], 16)

                if load:
                    def fetch(j, h, first):
                        k = j * 2 + h
                        if not first:
                            pool.wait_ge(sent[l][h], j * (16 * CH))
                        pool.dma_start(spos[:, h, :], posD[l][:, ds(k * CH, CH)]).then_inc(piece[l][h], 16)
                        pool.dma_start(srec[:, h, 0:CH * r], rec1[:, ds(k * (CH * r), CH * r)]).then_inc(piece[l][h], 16)

                    pool.wait_ge(pos_stored, 64)
                    for h in range(2):
                        pool.wait_ge(sent[0][h], 16 * CH * (PIECES // 2))
                    fetch(0, 0, True)
                    fetch(0, 1, True)
                    one(0, 0)
                    with loop(pool, 1, PIECES // 2) as j:
                        fetch(j, 0, False)
                        one(j - 1, 1)
                        fetch(j, 1, False)
                        one(j, 0)
                    one(PIECES // 2 - 1, 1)
                    for h in range(2):
                        pool.wait_ge(sent[l][h], 16 * CH * (PIECES // 2))
                else:
                    with loop(pool, 0, PIECES // 2) as j:
                        for h in range(2):
                            one(j, h)

            def gather(l):
                table = (hD, tD)[l]

                def one(it, s):
                    w = it * RSLOTS + s
                    pool.wait_ge(rec_in[l][s], (it + 1) * 16)
                    at_least(pool, (summed[0], v_add)[l], w - SLOTS + 1)
                    pool.sem_inc(pool_go, 1)
                    for c in range(2):
                        if l == 0:
                            dst, idx = xu[:, s % SLOTS, c, 0:F], rw0[:, s, c, 0:1]
                        else:
                            dst, idx = tb[:, s % SLOTS, c, :], rw1[:, s, c * R1:c * R1 + 1]
                        nc.gpsimd.indirect_dma_start(
                            out=dst, out_offset=None, in_=table,
                            in_offset=bass.IndirectOffsetOnAxis(ap=idx, axis=0)).then_inc(row_in[l][s % SLOTS], 16)

                window_turns(pool, one)

            scatter(0, False)
            pool.wait_ge(h_stored, 16)
            gather(0)
            scatter(1, True)
            pool.wait_ge(u_t_out, 16 * NB)
            pool.wait_ge(u_x2_out, 16 * NB)
            gather(1)

        @block.vector
        def _(dve):
            v = nc.vector

            class Steps:
                def __init__(self, s, start=0):
                    self.s, self.n, self.start = s, 0, start

                def inc(self, ins):
                    self.n += 1
                    ins.then_inc(self.s, 1)

                def link(self, ins):
                    self.inc(ins)
                    dve.wait_ge(self.s, self.start + self.n)

            c = Steps(dv)
            c.inc(v.memset(tail, 0))
            dve.wait_ge(dv, 1)
            for k in (1, R0 + 1, R1 + 1):
                v.memset(tail[:, k:k + 1], 2 * NN).then_inc(tail_ready, 1)

            def ranks(l):
                dve.wait_ge(in_key[l], 16)
                if l:
                    dve.wait_ge(pos_stored, 32)
                    dve.wait_ge(tabs_stored, 48)
                c.link(v.tensor_scalar(blki.bitcast(i32), keys.bitcast(i32), 7, None, ALU.arith_shift_right))
                c.link(v.tensor_copy(blkf, blki.bitcast(i32)))
                v.memset(junk[:, 2:3], 0.0).then_inc(dv_cnt[l], 1)
                with loop(dve, 0, NBE) as b:
                    dve.wait_ge(dv_cnt[l], b + 1)
                    v.tensor_scalar(eq[0], blkf, iota[:, ds(b, 1)], 0.0, ALU.is_equal, ALU.add,
                                    accum_out=cnt[:, ds(b, 1)]).then_inc(dv_cnt[l], 1)
                dve.wait_ge(dv_cnt[l], NBE + 1)
                c.inc(v.memset(junk[:, 0:1], 0.0))
                dve.wait_ge(dv, c.n)
                v.memset(junk[:, 0:1], 0.0).then_inc(cnt_ready, 1)
                dve.wait_ge(off_ready, l + 1)
                c.link(v.tensor_copy(tot, ps[:, 0, 64:64 + NBE]))
                c.link(v.tensor_tensor_scan(incl, ones[:, 0:NBE], tot, 0.0, ALU.mult, ALU.add))
                c.link(v.tensor_tensor(exc, incl, tot, ALU.subtract))
                c.link(v.tensor_tensor(off, exc, ps[:, 0, 0:NBE], ALU.add))
                c.link(v.tensor_scalar(off, off, -1.0, None, ALU.add))
                steps = 1
                for part, (lo, hi) in enumerate(((0, EARLY * CH), (EARLY * CH, EC))):
                    m = hi - lo
                    per = 4 - part
                    v.tensor_scalar(eq[0][:, 0:m], blkf[:, lo:hi], iota[:, 0:1], None, ALU.is_equal).then_inc(dv_rank[l], 1)
                    with loop(dve, 0, NBE // 2) as j:
                        for h in range(2):
                            b = j * 2 + h
                            k = j * (2 * per) + (h * per + steps)
                            dve.wait_ge(dv_rank[l], k)
                            v.tensor_tensor_scan(run[h][:, 0:m], ones[:, 0:1].to_broadcast((P, m)), eq[h][:, 0:m],
                                                 off[:, ds(b, 1)], ALU.mult, ALU.add).then_inc(dv_rank[l], 1)
                            dve.wait_ge(dv_rank[l], k + 1)
                            v.tensor_scalar(eq[1 - h][:, 0:m], blkf[:, lo:hi], iota[:, ds(b + 1, 1)], None,
                                            ALU.is_equal).then_inc(dv_rank[l], 1)
                            v.copy_predicated(rank[:, lo:hi], eq[h][:, 0:m].bitcast(i32), run[h][:, 0:m]).then_inc(dv_rank[l], 1)
                            if part == 0:
                                v.tensor_copy(off[:, ds(b, 1)], run[h][:, m - 1:m]).then_inc(dv_rank[l], 1)
                    steps += per * NBE
                    dve.wait_ge(dv_rank[l], steps)
                    steps += 1
                    v.tensor_copy(posi[:, lo:hi].bitcast(i32), rank[:, lo:hi]).then_inc(pos_ready, 1)
                c.link(v.tensor_scalar(nwin, tot, float(SW - 1), None, ALU.add))
                c.link(v.tensor_copy(nwi.bitcast(i32), nwin))
                c.link(v.tensor_scalar(nwi.bitcast(i32), nwi.bitcast(i32), SW.bit_length() - 1, None, ALU.arith_shift_right))
                c.link(v.tensor_copy(nwin, nwi.bitcast(i32)))
                c.link(v.tensor_tensor_scan(wend, ones[:, 0:NBE], nwin, 0.0, ALU.mult, ALU.add))
                c.link(v.scalar_tensor_tensor(pad, nwin, float(SW), tot, ALU.mult, ALU.subtract))
                for q in range(Q):
                    i = cst[:, C_WIN + q:C_WIN + q + 1]
                    c.link(v.tensor_scalar(mask[:, 0:NB], wend[:, 0:NB], i, None, ALU.is_le))
                    c.link(v.tensor_reduce(wb_[:, q:q + 1], mask[:, 0:NB], AX.X, ALU.add))
                    c.link(v.tensor_tensor(mask[:, 0:NB], mask[:, 0:NB], pad[:, 0:NB], ALU.mult))
                    c.link(v.tensor_reduce(wpad[:, q:q + 1], mask[:, 0:NB], AX.X, ALU.add))
                c.link(v.scalar_tensor_tensor(wst, cst[:, C_WIN:C_WIN + Q], float(SW), wpad, ALU.mult, ALU.subtract))
                c.link(v.tensor_scalar(wst, wst, float(EN), None, ALU.min))
                c.link(v.tensor_scalar(wb_, wb_, float(NB - 1), None, ALU.min))
                c.link(v.tensor_scalar(wbase, wb_, -float(P), None, ALU.mult))
                c.link(v.tensor_copy(wsti, wst))
                c.link(v.tensor_copy(wbi, wb_))
                v.memset(junk[:, 1:2], 0.0).then_inc(tabs_ready, 1)

            dve.wait_ge(in_c, 16)
            ranks(0)
            dve.wait_ge(in_ws, 32)
            c.link(v.tensor_tensor(ws[:, :], ws[:, :], scl, ALU.mult))
            dve.wait_ge(in_x, 16)
            with loop(dve, 0, NB) as b:
                v.bn_stats(stats[:, ds(b, 1), :].rearrange("p b s -> p (b s)"),
                           xs[:, ds(b, 1), :].rearrange("p b s -> p (b s)")).then_inc(dv_bn, 1)
            dve.wait_ge(dv_bn, NB)
            me, mo, ve, vo = (stats[:, :, k:k + 1].rearrange("p b s -> p (b s)") for k in (1, 4, 2, 5))
            c.link(v.tensor_tensor(mean, me, mo, ALU.add))
            c.link(v.tensor_scalar(mean, mean, 0.5, None, ALU.mult))
            c.link(v.tensor_tensor(tmpn, me, mean, ALU.subtract))
            c.link(v.tensor_tensor(tmpn, tmpn, tmpn, ALU.mult))
            c.link(v.tensor_tensor(var, ve, vo, ALU.add))
            c.link(v.tensor_scalar(var, var, 1.0 / F, EPS, ALU.mult, ALU.add))
            v.tensor_tensor(var, var, tmpn, ALU.add).then_inc(var_ready, 1)
            dve.wait_ge(std_ready, 1)
            c.link(v.reciprocal(rstd, tmpn))

            def over(a):
                return a.rearrange("p (b o) -> p b o", o=1).to_broadcast((P, NB, F))

            c.link(v.tensor_tensor(hS[:, :, :], xs, over(mean), ALU.subtract))
            c.link(v.tensor_tensor(hS[:, :, :], hS[:, :, :], over(rstd), ALU.mult))
            v.tensor_scalar(hS[:, :, :], hS[:, :, :], 0.0, None, ALU.max).then_inc(h_ready, 1)
            ranks(1)
            dve.wait_ge(pos_stored, 64)
            dve.wait_ge(tabs_stored, 96)
            dve.wait_ge(tail_stored, 32)
            dve.wait_ge(h_ready, 1)
            c.link(v.memset(acc[:, :], 0.0))
            dve.wait_ge(tab_in, 48)

            def rows_in(it, s):
                return (it * 2 + s // SLOTS + 1) * 32

            def one_hot(dst, s):
                return v.tensor_tensor(dst, iota.rearrange("p (o f) -> p o f", o=1).to_broadcast((P, 2, P)),
                                       keyf[:, s, :].rearrange("p (c o) -> p c o", o=1).to_broadcast((P, 2, P)), ALU.is_equal)

            def products(it, s):
                w, s4 = it * RSLOTS + s, s % SLOTS
                dve.wait_ge(row_in[0][s4], rows_in(it, s))
                dve.wait_ge(key_done[0], w + 1)
                one_hot(oh[:, s4, :, :], s).then_inc(built[0], 1)
                rr = rw0[:, s, :, 2:5].bitcast(f32)
                x0r = xu[:, s4, :, 2 * F:2 * F + 3 * S].rearrange("p c (k u) -> p c k u", k=3)
                v.tensor_tensor(x0r, xu[:, s4, :, 0:S].rearrange("p c (o u) -> p c o u", o=1).to_broadcast((P, 2, 3, S)),
                                rr.rearrange("p c (k o) -> p c k o", o=1).to_broadcast((P, 2, 3, S)), ALU.mult).then_inc(built[0], 1)
                x1r = xu[:, s4, :, 2 * F + 3 * S:A0].rearrange("p c (u k) -> p c u k", k=3)
                v.tensor_tensor(x1r, xu[:, s4, :, S:F].rearrange("p c (u k) -> p c u k", k=3),
                                rr.rearrange("p c (o k) -> p c o k", o=1).to_broadcast((P, 2, V, 3)), ALU.mult).then_inc(built[0], 1)

            def add(l, w, s):
                blk = dve.value_load(tab[0:1, ds(w + W, 1)], min_val=0, max_val=NB - 1)
                dve.wait_ge(summed[l], w + 1)
                at_least(dve, added[l], w)
                if l == 0:
                    a = acc[:, ds(blk * A0, A0)].rearrange("p (j f) -> p j f", j=2)
                    t = ps[:, 2 * (s % 2):2 * (s % 2) + 2, 0:HALF]
                else:
                    a, t = acc1[:, ds(blk * F, F)], ps[:, s % 2, 0:F]
                v.tensor_tensor(a, a, t, ALU.add).then_inc(added[l], 1)

            def edges0(it, s):
                products(it, s)
                if not (isinstance(it, int) and it == 0 and s == 0):
                    add(0, it * RSLOTS + s - 1, s - 1)

            window_turns(dve, edges0)
            add(0, W - 1, W - 1)
            dve.wait_ge(added[0], W)

            dve.wait_ge(wbig_in, 16)
            v.tensor_scalar(w000, w000, 5120.0 ** -0.5, None, ALU.mult).then_inc(w000_scaled, 1)

            U_DVE, U_FIN = 5, 7

            def finish(b, k, first=False):
                po = ps[:, 7, 0:F]
                if k == 0:
                    dve.wait_ge(u_x_in, (b + 1) * 16)
                    v.tensor_tensor(xb, xb, hS[:, ds(b, 1), :].rearrange("p b f -> p (b f)"), ALU.add).then_inc(u_fin, 1)
                elif k == 1:
                    dve.wait_ge(z0_mm, b * 8 + 8)
                    if not first:
                        dve.wait_ge(u_x2_out, b * 16)
                        dve.wait_ge(h2_done, b)
                    dve.wait_ge(u_dve, b * U_DVE + 5)
                    v.scalar_tensor_tensor(y[:, S:F].rearrange("p (w k) -> p k w", k=3),
                                           o1s.rearrange("p (k w) -> p k w", k=3), 1.0 / 64,
                                           po[:, S:F].rearrange("p (w k) -> p k w", k=3), ALU.mult, ALU.add).then_inc(u_fin, 1)
                    dve.wait_ge(u_fin, b * U_FIN + 1)
                    v.tensor_tensor(y[:, 0:S], po[:, 0:S], xb[:, 0:S], ALU.add).then_inc(u_fin, 1)
                elif k == 2:
                    dve.wait_ge(u_fin, b * U_FIN + 3)
                    v.tensor_tensor(y[:, S:F], y[:, S:F], xb[:, S:F], ALU.add).then_inc(y_done, 1)
                elif k == 3:
                    dve.wait_ge(y_done, b + 1)
                    v.memset(jk, 0.0).then_inc(u_fin, 1)
                    v.bn_stats(st6, y).then_inc(u_fin, 1)
                elif k == 4:
                    dve.wait_ge(u_fin, b * U_FIN + 5)
                    v.memset(jk, 0.0).then_inc(u_fin, 1)
                    v.bn_aggr(mv[:, 0:2], st6).then_inc(u_fin, 1)
                elif k == 5:
                    dve.wait_ge(u_fin, b * U_FIN + 7)
                    v.tensor_scalar(mv[:, 2:3], mv[:, 1:2], EPS, None, ALU.add).then_inc(u_var, 1)

            def normalised(b, k):
                if k == 0:
                    dve.wait_ge(u_std, b + 1)
                    v.reciprocal(mv[:, 3:4], mv[:, 2:3]).then_inc(u_norm, 1)
                elif k == 1:
                    dve.wait_ge(u_norm, b * 2 + 1)
                    v.tensor_scalar(hb, y, mv[:, 0:1], mv[:, 3:4], ALU.subtract, ALU.mult).then_inc(u_norm, 1)
                else:
                    dve.wait_ge(u_norm, b * 2 + 2)
                    v.tensor_scalar(hb, hb, 0.0, None, ALU.max).then_inc(h2_done, 1)

            def node(b, p, first=False):
                n = Steps(u_dve, b * U_DVE)

                def after(step):
                    dve.wait_ge(u_dve, n.start + step)

                x1 = hS[:, ds(b, 1), S:F].rearrange("p b (u k) -> p (b u) k", k=3)
                a1 = aS[p][:, S:F].rearrange("p (u k) -> p u k", k=3)

                def z0_product(j):
                    if j < 3:
                        dve.wait_ge(g_t, b * 2 + 2)
                    else:
                        dve.wait_ge(z0_t, b * 8 + j - 2)
                    v.tensor_tensor(pz[:, 512 * (j % 3):512 * (j % 3) + 512].rearrange("p (u v) -> p u v", v=S),
                                    hS[:, ds(b, 1), 8 * j:8 * j + 8].rearrange("p b (u o) -> p (b u) o", o=1).to_broadcast((P, 8, S)),
                                    aS[p][:, 0:S].rearrange("p (o v) -> p o v", o=1).to_broadcast((P, 8, S)),
                                    ALU.mult).then_inc(z0_prod, 1)

                def g_product(half):
                    if half:
                        dve.wait_ge(g_t, b * 2 + 1)
                    elif not first:
                        dve.wait_ge(z0_t, b * 8)
                    v.tensor_tensor(pz.rearrange("p (k u v) -> p k u v", k=3, v=V),
                                    x1[:, 16 * half:16 * half + 16, :].rearrange("p (u o) k -> p k u o", o=1).to_broadcast((P, 3, 16, V)),
                                    a1.rearrange("p (o v) k -> p k o v", o=1).to_broadcast((P, 3, 16, V)),
                                    ALU.mult).then_inc(g_made, 1)

                def g_sum(half):
                    dve.wait_ge(g_made, b * 2 + half + 1)
                    v.tensor_tensor(pz[:, 0:512], pz[:, 0:512], pz[:, 512:1024], ALU.add).then_inc(g_done, 1)

                def out1(u):
                    dve.wait_ge(z1_mm, b * 4 + u + 1)
                    if u:
                        after(u)
                    lo = 16 * (u // 2)
                    cf = (a1, x1)[u % 2][:, lo:lo + 16, :].rearrange("p (u o) k -> p k u o", o=1)
                    v.tensor_tensor(mb.rearrange("p (k j w) -> p k j w", k=3, w=V),
                                    ps[:, u % 2, :].rearrange("p (o j w) -> p o j w", o=1, w=V).to_broadcast((P, 3, 16, V)),
                                    cf.to_broadcast((P, 3, 16, V)), ALU.mult).then_inc(z1_used, 1)

                def out1_sum(u):
                    dve.wait_ge(z1_used, b * 4 + u + 1)
                    n.inc(v.tensor_reduce(o1[:, u * 3 * V:(u + 1) * 3 * V].rearrange("p (k w) -> p k w", k=3),
                                          mb.rearrange("p (k j w) -> p k w j", k=3, w=V), AX.X, ALU.add))

                def behind(part, k):
                    if not first:
                        part(b - 1, k)

                dve.wait_ge(agg_sb, b + 1)
                g_product(0)
                behind(finish, 0)
                g_sum(0)
                out1(0)
                if not first:
                    finish(b - 1, 1, isinstance(b, int) and b == 1)
                out1_sum(0)
                behind(finish, 2)
                g_product(1)
                behind(finish, 3)
                g_sum(1)
                out1(1)
                behind(finish, 4)
                out1_sum(1)
                behind(finish, 5)
                z0_product(0)
                z0_product(1)
                behind(normalised, 0)
                out1(2)
                behind(normalised, 1)
                z0_product(2)
                behind(normalised, 2)
                z0_product(3)
                out1_sum(2)
                z0_product(4)
                z0_product(5)
                out1(3)
                z0_product(6)
                z0_product(7)
                out1_sum(3)
                if not first:
                    dve.wait_ge(y_done, b)
                after(4)
                n.inc(v.tensor_reduce(o1s, o1.rearrange("p (u c) -> p c u", u=4), AX.X, ALU.add))
                assert n.n == U_DVE, n.n

            pairs(dve, node)
            for k in range(6):
                finish(NB - 1, k)
            for k in range(3):
                normalised(NB - 1, k)

            dve.wait_ge(tab_in, 96)
            dve.wait_ge(h2_kept, NB)
            c.link(v.memset(acc1, 0.0))

            def factors(it, s):
                w, s4, t2 = it * RSLOTS + s, s % SLOTS, s % 2
                ev = rw1[:, s, :].rearrange("p (c r) -> p c r", c=2)[:, :, 3:6].bitcast(f32)
                ev = ev.rearrange("p c (o d) -> p c o d", o=1).to_broadcast((P, 2, V, 3))
                dve.wait_ge(row_in[1][s4], rows_in(it, s))
                at_least(dve, z_sum, w)
                v.tensor_tensor(zq, tb[:, s4, :, TM + S:TW].rearrange("p c (v d) -> p c v d", d=3), ev, ALU.mult).then_inc(z_in, 1)
                at_least(dve, v_add, w)
                v.tensor_tensor(vq, tb[:, s4, :, 0:V].rearrange("p c (v o) -> p c v o", o=1).to_broadcast((P, 2, V, 3)),
                                ev, ALU.mult).then_inc(z_in, 1)
                dve.wait_ge(z_in, w * 2 + 1)
                at_least(dve, z_t, w - 1)
                v.tensor_reduce(sc[:, t2, :, 160:192], zq, AX.X, ALU.add).then_inc(z_sum, 1)
                dve.wait_ge(key_done[1], w + 1)
                at_least(dve, summed[1], w - SLOTS + 1)
                one_hot(oh1[:, s4, :, :], s).then_inc(built[1], 1)
                dve.wait_ge(z_in, w * 2 + 2)
                dve.wait_ge(scaled[1], (w + 1) * 2)
                v.tensor_tensor(mg[:, s4, :, S:F], vq.rearrange("p c v d -> p c (v d)"), sc[:, t2, :, 0:3 * V],
                                ALU.add).then_inc(v_add, 1)

            def gated(w, s):
                s4, t2 = s % SLOTS, s % 2
                dve.wait_ge(gate_done, w + 1)
                dve.wait_ge(z_mm, w + 1)
                v.tensor_tensor(mg[:, s4, :, 0:S], ps[:, 6 + t2, 0:2 * S].rearrange("p (c u) -> p c u", c=2),
                                gt[:, s4, :, 0:S], ALU.mult).then_inc(msg, 1)
                dve.wait_ge(v_add, w + 1)
                v.tensor_tensor(mg[:, s4, :, S:F], mg[:, s4, :, S:F], gt[:, s4, :, S:F], ALU.mult).then_inc(msg, 1)

            def edges1(it, s):
                w = it * RSLOTS + s
                start = isinstance(it, int) and it == 0
                factors(it, s)
                if not (start and s < 1):
                    gated(w - 1, s - 1)
                if not (start and s < 2):
                    add(1, w - 2, s - 2)

            window_turns(dve, edges1)
            gated(W - 1, W - 1)
            add(1, W - 2, W - 2)
            add(1, W - 1, W - 1)
            dve.wait_ge(added[1], W)

            def total(b, p, i):
                dve.wait_ge(f_mm, b + 1)
                dve.wait_ge(f_x_in[p], i * 16 + 16)
                at_least(dve, f_out[p], i * 16)
                v.tensor_tensor(fo[p], ps[:, 6 + p, 0:F], fx[p], ALU.add).then_inc(f_done, 1)

            def sum_h(b, p):
                at_least(dve, f_t, b - 1)
                v.tensor_tensor(fh[p], acc1[:, ds(b * F, F)], hS[:, ds(b, 1), :].rearrange("p b f -> p (b f)"),
                                ALU.add).then_inc(f_add, 1)

            def next_sum(b, p, i):
                if not (isinstance(b, int) and b == NB - 1):
                    sum_h(b + 1, 1 - p)

            sum_h(0, 0)
            output_pairs(dve, next_sum, total)

        @block.scalar
        def _(act):
            a = nc.scalar
            act.wait_ge(var_ready, 1)
            a.activation(tmpn, var, ACT.Sqrt).then_inc(std_ready, 1)
            act.wait_ge(pos_ready, 1)
            act.dma_start(keys.bitcast(i32), key1).then_inc(in_key[1], 16)
            act.wait_ge(h_ready, 1)
            act.dma_start(hD.rearrange("(b p) f -> p b f", p=P), hS[:, :, :]).then_inc(h_stored, 16)

            def key(l, w, s, rec, turn):
                act.wait_ge(rec_in[l][s], (turn + 1) * 16)
                at_least(act, built[l], (3, 1)[l] * (w - RSLOTS + 1))
                a.activation(keyf[:, s, :], rec, ACT.Identity, bias=base[:, ds(w, 1)]).then_inc(key_done[l], 1)

            def dist(it, s):
                s4 = s % SLOTS
                key(0, it * RSLOTS + s, s, rw0[:, s, :, 1:2].rearrange("p c o -> p (c o)"), it)
                act.wait_ge(row_in[0][s4], (it * 2 + s // SLOTS + 1) * 32)
                for cc in range(2):
                    a.activation(xu[:, s4, cc, F:2 * F], xu[:, s4, cc, 0:F], ACT.Copy,
                                 scale=rw0[:, s, cc, 5:6].bitcast(f32)).then_inc(scaled[0], 1)

            act.wait_ge(tab_in, 48)
            window_turns(act, dist)

            def copy_sums(b, first=False):
                h = hS[:, ds(b, 1), :].rearrange("p b f -> p (b f)")
                if not first:
                    act.wait_ge(agg_mm, b)
                    act.wait_ge(h_t, b)
                a.activation(ab, acc[:, ds(b * A0, A0)], ACT.Copy).then_inc(agg_c, 1)
                a.activation(x1b, h[:, S:F], ACT.Copy)
                a.activation(cat[:, S:2 * S], h[:, 0:S], ACT.Copy)
                act.wait_ge(agg_t, b + 1)
                a.activation(aT[:, 0:4 * P], ps[:, 5, :], ACT.Copy)
                a.activation(aT[0:A0 - 4 * P, 4 * P:5 * P], ps[0:A0 - 4 * P, 6, 0:P], ACT.Copy).then_inc(agg_t_sb, 1)

            def copy_aggregates(b, p, first=False):
                act.wait_ge(agg_mm, b + 1)
                a.activation(cat[:, 0:S], ps[:, 5, 0:S], ACT.Copy)
                if not first:
                    act.wait_ge(z1_used, b * 4 - 4)
                    act.wait_ge(z0_mm, b * 8 - 8)
                a.activation(aS[p], ps[:, 5, 0:F], ACT.Copy).then_inc(agg_sb, 1)

            def copy_factors(b, p):
                act.wait_ge(h_t, b + 1)
                a.activation(catT[p], ps[:, 6, 0:P], ACT.Copy)
                a.activation(x1T[p][0:3 * V, :], ps[0:3 * V, 6, P:2 * P], ACT.Copy).then_inc(h_t_sb, 1)

            def std(b):
                act.wait_ge(u_var, b + 1)
                a.activation(mv[:, 2:3], mv[:, 2:3], ACT.Sqrt).then_inc(u_std, 1)

            def copy_h2(b):
                act.wait_ge(h2_t, b + 1)
                a.activation(hT[:, 0:P], ps[:, 5, 0:P], ACT.Copy)
                a.activation(hT[0:V, P:2 * P], ps[0:V, 5, P:2 * P], ACT.Copy).then_inc(h2_t_sb, 1)
                a.activation(hS[:, ds(b, 1), :].rearrange("p b f -> p (b f)"), hb, ACT.Copy).then_inc(h2_kept, 1)

            def copy_rows(b, first=False):
                act.wait_ge(t_mm, b + 1)
                if not first:
                    act.wait_ge(u_t_out, b * 16)
                a.activation(tS[:, TM:TW], hb, ACT.Copy)
                a.activation(tS[:, 0:TM], ps[:, 6, 0:TM], ACT.Copy).then_inc(t_sb, 1)

            def node(b, p, first=False):
                last = isinstance(b, int) and b == NB - 1
                def g_copy(half):
                    act.wait_ge(g_t, b * 2 + half + 1)
                    if not first:
                        act.wait_ge(z0_mm, b * 8)
                    a.activation(gT[:, half * 512:half * 512 + 512], ps[:, 4, :], ACT.Copy).then_inc(g_t_sb, 1)

                def z0_copy(j):
                    act.wait_ge(z0_t, b * 8 + j + 1)
                    if not (first and j < 2):
                        act.wait_ge(z0_mm, b * 8 + j - 1)
                    a.activation(cT[j % 2], ps[:, 2 + j % 2, :], ACT.Copy).then_inc(z0_t_sb, 1)

                if not last:
                    copy_sums(b + 1)
                g_copy(0)
                if not last:
                    copy_aggregates(b + 1, 1 - p, first)
                g_copy(1)
                if not last:
                    copy_factors(b + 1, 1 - p)
                if not first:
                    std(b - 1)
                else:
                    act.wait_ge(agg_c, 2)
                for j in range(8):
                    z0_copy(j)
                    if j == 3 and not first:
                        copy_h2(b - 1)
                    if j == 5 and not first:
                        copy_rows(b - 1, isinstance(b, int) and b == 1)

            act.wait_ge(added[0], W)
            copy_sums(0, True)
            copy_aggregates(0, 0, True)
            copy_factors(0, 0)
            pairs(act, node)
            std(NB - 1)
            copy_h2(NB - 1)
            copy_rows(NB - 1)

            def key_of(turn, w, s):
                key(1, w, s, rw1[:, s, :].rearrange("p (c r) -> p c r", c=2)[:, :, 1:2].rearrange("p c o -> p (c o)"), turn)

            def attributes(w, s):
                act.wait_ge(attr_t, w + 1)
                at_least(act, gate_mm, w - 1)
                a.activation(atr[0:2 * R1, s % 2, :], ps[0:2 * R1, 4, 0:P], ACT.Copy).then_inc(attr_c, 1)

            def gates(w, s):
                act.wait_ge(gate_mm, w + 1)
                at_least(act, msg, 2 * (w - SLOTS + 1))
                a.activation(gt[:, s % SLOTS, :, :], ps[:, 2:4, 0:F], ACT.Sigmoid).then_inc(gate_done, 1)

            def edges1(it, s):
                w, s4, t2 = it * RSLOTS + s, s % SLOTS, s % 2
                nxt = not (isinstance(it, int) and w == W - 1)
                act.wait_ge(row_in[1][s4], (it * 2 + s // SLOTS + 1) * 32)
                at_least(act, z_t, w - 1)
                at_least(act, v_add, w - 1)
                for cc in range(2):
                    a.activation(sc[:, t2, cc, 0:160], tb[:, s4, cc, V:V + 160], ACT.Copy,
                                 scale=rw1[:, s, cc * R1 + 2:cc * R1 + 3].bitcast(f32)).then_inc(scaled[1], 1)
                if nxt:
                    key_of(it + (s + 1) // RSLOTS, w + 1, (s + 1) % RSLOTS)
                    attributes(w + 1, s + 1)
                act.wait_ge(z_t, w + 1)
                at_least(act, z_mm, w - 1)
                a.activation(zT[0:S + V, t2, :], ps[0:S + V, 5, 0:2 * P], ACT.Copy).then_inc(z_t_sb, 1)
                if nxt:
                    gates(w + 1, s + 1)

            act.wait_ge(tab_in, 96)
            key_of(0, 0, 0)
            attributes(0, 0)
            gates(0, 0)
            window_turns(act, edges1)

            def sum_t(b, p, i):
                act.wait_ge(f_t, b + 1)
                at_least(act, f_mm, b - 1)
                a.activation(fT[p][:, 0:P], ps[:, 4 + p, 0:P], ACT.Copy)
                a.activation(fT[p][0:V, P:2 * P], ps[0:V, 4 + p, P:2 * P], ACT.Copy).then_inc(f_t_sb, 1)

            output_pairs(act, sum_t, lambda b, p, i: None)

        @block.tensor
        def _(pe):
            t = nc.tensor

            def flip(dst, src):
                return t.matmul(dst, src, ident, start=True, stop=True)

            def turn(dst, src):
                return t.transpose(dst, src, ident)

            pe.wait_ge(in_c, 16)
            for l in range(2):
                pe.wait_ge(cnt_ready, l + 1)
                t.matmul(ps[:, 0, 0:NBE], tri, cnt, start=True, stop=True)
                t.matmul(ps[:, 0, 64:64 + NBE], ones, cnt, start=True, stop=True).then_inc(off_ready, 1)

            def sums(it, s):
                w, s4 = it * RSLOTS + s, s % SLOTS
                pe.wait_ge(built[0], (w + 1) * 3)
                pe.wait_ge(scaled[0], (w + 1) * 2)
                at_least(pe, added[0], w - 1)
                for cc in range(2):
                    for j in range(2):
                        last = t.matmul(ps[:, 2 * (s % 2) + j, 0:HALF], oh[:, s4, cc, :],
                                        xu[:, s4, cc, j * HALF:(j + 1) * HALF], start=(cc == 0), stop=(cc == 1))
                last.then_inc(summed[0], 1)

            window_turns(pe, sums)

            pe.wait_ge(added[0], W)
            pe.wait_ge(wbig_in, 16)

            def sums_t(b):
                pe.wait_ge(agg_c, b + 1)
                for k in range(KC):
                    n = min(P, A0 - k * P)
                    last = turn(ps[0:n, 5 + k // 4, (k % 4) * P:(k % 4) * P + P], ab[:, k * P:k * P + n])
                last.then_inc(agg_t, 1)

            def aggregate(b):
                pe.wait_ge(agg_t_sb, b + 1)
                for k in range(KC):
                    n = min(P, A0 - k * P)
                    last = t.matmul(ps[:, 5, 0:F], aT[0:n, k * P:(k + 1) * P], ws[0:n, WB + k * F:WB + (k + 1) * F],
                                    start=(k == 0), stop=(k == KC - 1))
                last.then_inc(agg_mm, 1)

            def factors_t(b):
                pe.wait_ge(agg_sb, b + 1)
                turn(ps[:, 6, 0:P], cat)
                turn(ps[0:3 * V, 6, P:2 * P], x1b).then_inc(h_t, 1)

            def h2_flips(b):
                pe.wait_ge(h2_done, b + 1)
                turn(ps[:, 5, 0:P], hb[:, 0:P])
                turn(ps[0:V, 5, P:2 * P], hb[:, P:F]).then_inc(h2_t, 1)

            def rows(b):
                pe.wait_ge(h2_t_sb, b + 1)
                t.matmul(ps[:, 6, 0:TM], hT[:, 0:P], ws[:, WT:WT + TM], start=True, stop=False)
                t.matmul(ps[:, 6, 0:TM], hT[0:V, P:2 * P], ws[0:V, WT + TM:WT + 2 * TM], start=False, stop=True).then_inc(t_mm, 1)

            def z1(b, p, u, first=False):
                if not first:
                    pe.wait_ge(z1_used, b * 4 + u - 1)
                lo = (S, 0)[u % 2]
                t.matmul(ps[:, u % 2, :], catT[p][lo:lo + S, :], w1x1[lo:lo + S, (u // 2) * 512:(u // 2) * 512 + 512],
                         start=True, stop=True).then_inc(z1_mm, 1)

            def node(b, p, first=False):
                last_block = isinstance(b, int) and b == NB - 1

                def g_turned(half):
                    pe.wait_ge(g_done, b * 2 + half + 1)
                    if half or not first:
                        pe.wait_ge(g_t_sb, b * 2 + half)
                    for c in range(4):
                        for k in (0, 2):
                            last = t.matmul(ps[:, 4, c * P:c * P + P], pz[:, k * 512 + c * P:k * 512 + c * P + P], ident,
                                            start=(k == 0), stop=(k == 2))
                    last.then_inc(g_t, 1)

                def z0_turned(j):
                    pe.wait_ge(z0_prod, b * 8 + j + 1)
                    if not (first and j < 2):
                        pe.wait_ge(z0_t_sb, b * 8 + j - 1)
                    for c in range(4):
                        last = turn(ps[:, 2 + j % 2, c * P:c * P + P], pz[:, 512 * (j % 3) + c * P:512 * (j % 3) + c * P + P])
                    last.then_inc(z0_t, 1)

                def z0_product(j):
                    pe.wait_ge(z0_t_sb, b * 8 + j + 1)
                    for c in range(4):
                        m = j * 4 + c
                        last = t.matmul(ps[:, 7, 0:S], cT[j % 2][:, c * P:c * P + P], w000[:, m * S:(m + 1) * S],
                                        start=False, stop=(m == 31))
                    last.then_inc(z0_mm, 1)

                if not last_block:
                    if not first and not (isinstance(b, int) and b == 1):
                        pe.wait_ge(t_sb, b - 1)
                    sums_t(b + 1)
                g_turned(0)
                if not last_block:
                    aggregate(b + 1)
                g_turned(1)
                if not last_block:
                    factors_t(b + 1)
                else:
                    pe.wait_ge(t_sb, b - 1)
                z1(b, p, 2)
                z0_turned(0)
                z0_turned(1)
                z1(b, p, 3)
                z0_turned(2)
                if not first:
                    pe.wait_ge(y_done, b)
                t.matmul(ps[:, 7, S:F], x1T[p][0:3 * V, :], ws[0:3 * V, WU + S:WU + F], start=True, stop=True)
                t.matmul(ps[:, 7, 0:S], catT[p][S:P, :], ws[S:P, WU:WU + S], start=True, stop=False)
                pe.wait_ge(g_t_sb, b * 2 + 2)
                for k in range(8):
                    t.matmul(ps[:, 7, 0:S], gT[:, k * P:(k + 1) * P], ws[:, W110 + k * S:W110 + (k + 1) * S],
                             start=False, stop=False)
                if first:
                    pe.wait_ge(w000_scaled, 1)
                for j in range(8):
                    z0_product(j)
                    if j == 5 and not last_block:
                        pe.wait_ge(h_t_sb, b + 2)
                        z1(b + 1, 1 - p, 0)
                        z1(b + 1, 1 - p, 1)
                    if j < 5:
                        z0_turned(j + 3)
                    if j == 1 and not first:
                        h2_flips(b - 1)
                    if j == 2 and not first:
                        if not last_block:
                            pe.wait_ge(h_t_sb, b + 2)
                        rows(b - 1)

            sums_t(0)
            aggregate(0)
            factors_t(0)
            pe.wait_ge(h_t_sb, 1)
            z1(0, 0, 0, True)
            z1(0, 0, 1, True)
            pairs(pe, node)
            pe.wait_ge(t_sb, NB - 1)
            h2_flips(NB - 1)
            rows(NB - 1)

            def attributes(it, w, s):
                pe.wait_ge(rec_in[1][s], (it + 1) * 16)
                at_least(pe, attr_c, w)
                flip(ps[0:2 * R1, 4, 0:P], rw1[:, s, :].bitcast(f32)).then_inc(attr_t, 1)

            def gate(w, s):
                pe.wait_ge(attr_c, w + 1)
                at_least(pe, gate_done, w)
                for cc in range(2):
                    k = slice(cc * R1, (cc + 1) * R1)
                    last = t.matmul(ps[:, 2 + cc, 0:F], atr[k, s % 2, :], ws[k, WG:WG + F], start=True, stop=True)
                last.then_inc(gate_mm, 1)

            def sums1(w, s):
                pe.wait_ge(msg, 2 * (w + 1))
                pe.wait_ge(built[1], w + 1)
                at_least(pe, added[1], w - 1)
                for cc in range(2):
                    last = t.matmul(ps[:, s % 2, 0:F], oh1[:, s % SLOTS, cc, :], mg[:, s % SLOTS, cc, :],
                                    start=(cc == 0), stop=(cc == 1))
                last.then_inc(summed[1], 1)

            def edges1(it, s):
                w, t2 = it * RSLOTS + s, s % 2
                nxt = not (isinstance(it, int) and w == W - 1)
                if nxt:
                    attributes(it + (s + 1) // RSLOTS, w + 1, (s + 1) % RSLOTS)
                pe.wait_ge(scaled[1], (w + 1) * 2)
                pe.wait_ge(z_sum, w + 1)
                at_least(pe, z_t_sb, w)
                for cc in range(2):
                    last = flip(ps[0:S + V, 5, cc * P:(cc + 1) * P], sc[:, t2, cc, 96:192])
                last.then_inc(z_t, 1)
                if nxt:
                    gate(w + 1, s + 1)
                pe.wait_ge(z_t_sb, w + 1)
                at_least(pe, msg, 2 * (w - 1))
                for cc in range(2):
                    last = t.matmul(ps[:, 6 + t2, cc * S:(cc + 1) * S], zT[0:S + V, t2, cc * P:(cc + 1) * P],
                                    ws[0:S + V, WZ:WZ + S], start=True, stop=True)
                last.then_inc(z_mm, 1)
                if not (isinstance(it, int) and w == 0):
                    sums1(w - 1, s - 1)

            pe.wait_ge(t_sb, NB)
            attributes(0, 0, 0)
            gate(0, 0)
            window_turns(pe, edges1)
            sums1(W - 1, W - 1)

            def product(b, p, i):
                pe.wait_ge(f_t_sb, b + 1)
                at_least(pe, f_done, b - 1)
                t.matmul(ps[:, 6 + p, 0:F], fT[p][:, 0:P], ws[:, WF:WF + F], start=True, stop=False)
                t.matmul(ps[:, 6 + p, 0:F], fT[p][0:V, P:2 * P], ws[0:V, WF + F:WF + 2 * F], start=False, stop=True).then_inc(f_mm, 1)

            def sum_t(b, p, i):
                pe.wait_ge(f_add, b + 1)
                at_least(pe, f_t_sb, b - 1)
                flip(ps[:, 4 + p, 0:P], fh[p][:, 0:P])
                flip(ps[0:V, 4 + p, P:2 * P], fh[p][:, P:F]).then_inc(f_t, 1)

            pe.wait_ge(gate_done, W)
            output_pairs(pe, sum_t, product)


_ORDER = ["x", "rec0", "rec1", "key0", "key1", "wsmall", "wscale", "wbig", "const"]


def constants():
    c = np.zeros((P, CW), np.float32)
    c[:, C_ID:C_ID + P] = np.eye(P)
    c[:, C_TRI:C_TRI + P] = np.triu(np.ones((P, P)), 1)
    c[:, C_ONE:C_ONE + P] = 1.0
    c[:, C_IOTA:C_IOTA + P] = np.arange(P)
    c[:, C_WIN:C_WIN + Q] = np.arange(Q * P).reshape(Q, P).T
    return c


def place(ws, w000, w011, w101, w110, lm0, lm1, m000, m011, m101, m110, lu0, lu1, ss, sv, vs, vv, rad, bias, ls, lv):
    full = np.zeros((KC * P, F), np.float32)
    full[0:S, 0:S] = lm0
    full[F:F + S, 0:S] = m000
    for k in range(3):
        full[S + k:F:3, S + k::3] = lm1
        full[F + S + k:2 * F:3, S + k::3] = m101
        full[2 * F + k * S:2 * F + (k + 1) * S, S + k::3] = m011
        full[2 * F + 3 * S + k:A0:3, 0:S] = m110
    for k in range(KC):
        ws[:, WB + k * F:WB + (k + 1) * F] = full[k * P:(k + 1) * P]

    def two(at, m, n):
        ws[:, at:at + n] = m[0:P]
        ws[0:V, at + n:at + 2 * n] = m[P:F]

    t = np.zeros((F, TM), np.float32)
    t[0:S, 0:V] = sv
    for k in range(3):
        t[S + k::3, V + k::3] = vs
    two(WT, t, TM)
    ws[0:S, WZ:WZ + S], ws[S:S + V, WZ:WZ + S] = ss, vv
    u = np.zeros((F, F), np.float32)
    u[0:S, 0:S] = lu0
    f = np.zeros((F, F), np.float32)
    f[0:S, 0:S] = ls
    for k in range(3):
        u[S + k::3, S + k::3] = lu1
        f[S + k::3, S + k::3] = lv
    ws[S:P, WU:WU + S] = u[0:S, 0:S]
    ws[0:3 * V, WU + S:WU + F] = u[S:F, S:F]
    two(WF, f, F)
    for c in range(2):
        ws[c * R1 + 6:c * R1 + 22, WG:WG + F] = rad.T
        ws[c * R1 + 22, WG:WG + F] = bias
    for c in range(8):
        ws[:, W110 + c * S:W110 + (c + 1) * S] = w110[c * P:(c + 1) * P]


def kernel(**inputs):
    import numpy as _np
    import concourse.bacc as _bacc
    from concourse import mybir as _mybir
    from concourse.bass_utils import run_bass_kernel_spmd as _run

    g = {k: _np.asarray(a) for k, a in inputs.items()}
    one = lambda shape, value: _np.full(shape, value, _np.float32)
    x = _np.zeros((NN, F), _np.float32)
    x[0:N] = g["x"]
    src = _np.full((EN,), NN - 1, _np.int32)
    dst = _np.full((EN,), NN - 1, _np.int32)
    src[0:E], dst[0:E] = g["src"], g["dst"]
    rec1 = _np.zeros((EN, R1), _np.int32)
    rec1[:, 0], rec1[:, 1] = src, dst
    rec1[0:E, 2:6] = g["edge_attr_4"].view(_np.int32)
    rec1[0:E, 6:22] = g["edge_attr_16"].view(_np.int32)
    rec1[:, 22] = _np.ones((EN,), _np.float32).view(_np.int32)
    rec0 = _np.zeros((EN, R0), _np.int32)
    rec0[:, 0], rec0[:, 1] = dst, src
    rec0[0:E, 2:6] = g["edge_attr_4"].view(_np.int32)
    p0, p1 = "L0_gnn_", "L1_gnn_"
    wsmall, wscale = _np.zeros((P, WS), _np.float32), _np.zeros((P, WS), _np.float32)
    r2, r3 = 2.0 ** -0.5, 3.0 ** -0.5
    place(wsmall, None, None, None, g[p0 + "wu110"].reshape(V * V, S), g[p0 + "lm0"], g[p0 + "lm1"],
          g[p0 + "wm000"][:, 0], g[p0 + "wm011"][:, 0], g[p0 + "wm101"][:, 0], g[p0 + "wm110"][:, 0],
          g[p0 + "lu0"], g[p0 + "lu1"], g[p1 + "W_ss"], g[p1 + "W_sv"], g[p1 + "W_vs"], g[p1 + "W_vv"],
          g[p1 + "W_rad"], g[p1 + "b_rad"], g[p1 + "L_s"], g[p1 + "L_v"])
    m = (S + V) ** -0.5
    place(wscale, None, None, None, one((V * V, S), r3 * 5120.0 ** -0.5), S ** -0.5, V ** -0.5, m, m, m, m * r3,
          S ** -0.5, V ** -0.5, r2 * S ** -0.5, r2 * r3 * S ** -0.5, r2 * r3 * V ** -0.5, r2 * r3 * V ** -0.5,
          one((F, 16), 1.0), one((F,), 1.0), S ** -0.5, V ** -0.5)
    half = S * S // 2
    wbig = _np.zeros((P, half + V * V), _np.float32)
    wbig[:, 0:half] = g[p0 + "wu000"].reshape(S * S // P, P, S).transpose(1, 0, 2).reshape(P, half)
    wbig[0:S, half:] = g[p0 + "wu101"].transpose(1, 0, 2).reshape(S, V * V)
    wbig[S:P, half:] = g[p0 + "wu011"].reshape(S, V * V)
    arrays = {"x": x, "rec0": rec0.reshape(P, EC * R0), "rec1": rec1.reshape(P, EC * R1), "key0": src.reshape(P, EC),
              "key1": dst.reshape(P, EC), "wsmall": wsmall, "wscale": wscale, "wbig": wbig, "const": constants()}
    nc = _bacc.Bacc("TRN2", target_bir_lowering=False, num_devices=1)
    args = [nc.dram_tensor(f"in_{n}", arrays[n].shape, _mybir.dt.from_np(arrays[n].dtype), kind="ExternalInput").ap()
            for n in _ORDER]
    o = nc.dram_tensor("out_0", (NN, F), _mybir.dt.float32, kind="ExternalOutput").ap()
    program(nc, *args, o)
    r = _run(nc, [{f"in_{n}": arrays[n] for n in _ORDER}], core_ids=[0])
    return r.results[0]["out_0"][0:N]
```
